# Optimizing a Trainium2 kernel written in Bass

```python
import numpy as np
import jax
import jax.numpy as jnp

def _softmax(x, axis=-1):
    return jax.nn.softmax(x, axis=axis)

def _gelu(x):
    return jax.nn.gelu(x, approximate=True)

def _silu(x):
    return jax.nn.silu(x)

def _sigmoid(x):
    return jax.nn.sigmoid(x)

def _layernorm(x, axis=-1, eps=1e-05):
    m = jnp.mean(x, axis=axis, keepdims=True)
    v = jnp.var(x, axis=axis, keepdims=True)
    return (x - m) / jnp.sqrt(v + eps)

def _scatter_add(tgt, idx, src, axis=0):
    return tgt.at[idx].add(src)

def _segment_sum(src, seg, n):
    return jax.ops.segment_sum(src, seg, n)
kernel_name = 'mk_seq_postln_d2_jaxref_r4_c0d7a4'

def setup_inputs(seed: int=0):
    np.random.seed(seed)
    _w = jnp.asarray

    def _L0_attn_setup():
        import jax, jax.numpy as jnp
        import numpy as np
        D_MODEL = 256
        N_HEADS = 16
        D_HEAD = D_MODEL // N_HEADS
        SCALE = 1.0 / np.sqrt(D_HEAD).astype(np.float32)

        def _feature_map(x):
            return jax.nn.elu(x) + 1.0
        key = jax.random.key(seed)
        ks = jax.random.split(key, 7)
        b, s = (4, 512)
        w = 1.0 / np.sqrt(D_MODEL).astype(np.float32)
        return {'x': jax.random.normal(ks[0], (b, s, D_MODEL), dtype=jnp.float32), 'Wq': jax.random.normal(ks[1], (D_MODEL, D_MODEL), dtype=jnp.float32) * w, 'Wk': jax.random.normal(ks[2], (D_MODEL, D_MODEL), dtype=jnp.float32) * w, 'Wv': jax.random.normal(ks[3], (D_MODEL, D_MODEL), dtype=jnp.float32) * w, 'Wo': jax.random.normal(ks[4], (D_MODEL, D_MODEL), dtype=jnp.float32) * w, 'Wg': jax.random.normal(ks[5], (N_HEADS, D_MODEL), dtype=jnp.float32) * w, 'bg': jax.random.normal(ks[6], (N_HEADS,), dtype=jnp.float32) * 0.02}
    _L0_attn_in = _L0_attn_setup()

    def _L0_ffn_setup():
        import jax, jax.numpy as jnp
        import numpy as np
        TOP_K = 2
        E = 8
        D = 256
        F = 512
        B, S = (2, 256)
        key = jax.random.key(seed)
        ks = jax.random.split(key, 8)
        sc = 0.02
        return {'x_bsD': jax.random.normal(ks[0], (B, S, D), dtype=jnp.float32), 'router_DE': jax.random.normal(ks[1], (D, E), dtype=jnp.float32) * sc, 'w_in_shared_FD': jax.random.normal(ks[2], (F, D), dtype=jnp.float32) * sc, 'w_out_shared_DF': jax.random.normal(ks[3], (D, F), dtype=jnp.float32) * sc, 'w_swiglu_FD': jax.random.normal(ks[4], (F, D), dtype=jnp.float32) * sc, 'w_in_eDF': jax.random.normal(ks[5], (E, D, F), dtype=jnp.float32) * sc, 'w_swiglu_eDF': jax.random.normal(ks[6], (E, D, F), dtype=jnp.float32) * sc, 'w_out_eFD': jax.random.normal(ks[7], (E, F, D), dtype=jnp.float32) * sc}
    _L0_ffn_in = _L0_ffn_setup()

    def _L1_attn_setup():
        import jax, jax.numpy as jnp
        import numpy as np
        D = 256
        B, S = (4, 1024)
        LR = 0.01
        WD = 0.01
        MAX_ALR = 0.1
        EPS = 1e-08

        def _lmm(params, h):
            for W, b in params:
                h = h + jax.nn.silu(h @ W + b)
            return h

        def _reference_tuple_inner(x, Wk, bk, Wq, bq, Wv, bv, Wlr, blr, W1, b1, W2, b2):
            keys = x @ Wk + bk
            queries = x @ Wq + bq
            values = x @ Wv + bv
            alr = MAX_ALR * jax.nn.sigmoid(x @ Wlr + blr).reshape(-1)
            kf = keys.reshape(-1, D)
            vf = values.reshape(-1, D)
            params = ((W1, b1), (W2, b2))

            def loss_fn(ps):
                pred = _lmm(ps, kf)
                per_tok = jnp.mean((pred - vf) ** 2, axis=-1)
                return jnp.sum(per_tok * alr)
            grads = jax.grad(loss_fn)(params)

            def adamw(p, g):
                return p * (1.0 - LR * WD) - LR * g / (jnp.sqrt(g * g) + EPS)
            new_params = jax.tree_util.tree_map(adamw, params, grads)
            retrieved = _lmm(new_params, queries)
            surprises = jax.tree_util.tree_map(lambda g: -g, grads)
            return (retrieved, *jax.tree_util.tree_leaves(surprises))
        key = jax.random.key(seed)
        ks = jax.random.split(key, 13)
        s = 1.0 / np.sqrt(D)

        def lin(k, shape):
            return jax.random.uniform(k, shape, minval=-s, maxval=s, dtype=jnp.float32)
        return {'x': jax.random.normal(ks[0], (B, S, D), dtype=jnp.float32), 'Wk': lin(ks[1], (D, D)), 'bk': lin(ks[2], (D,)), 'Wq': lin(ks[3], (D, D)), 'bq': lin(ks[4], (D,)), 'Wv': lin(ks[5], (D, D)), 'bv': lin(ks[6], (D,)), 'Wlr': lin(ks[7], (D, 1)), 'blr': lin(ks[8], (1,)), 'W1': lin(ks[9], (D, D)), 'b1': lin(ks[10], (D,)), 'W2': lin(ks[11], (D, D)), 'b2': lin(ks[12], (D,))}
    _L1_attn_in = _L1_attn_setup()

    def _L1_ffn_setup():
        import jax, jax.numpy as jnp
        import numpy as np
        EPS = 1e-05

        def _quantize(W):
            gamma = jnp.mean(jnp.abs(W))
            return jnp.clip(jnp.round(W / (gamma + EPS)), -1.0, 1.0)
        key = jax.random.key(seed)
        k_x, k_w1, k_b1, k_w2, k_b2 = jax.random.split(key, 5)
        n_embd = 256
        d_ff = 4 * n_embd
        B, S = (4, 1024)
        bound1 = 1.0 / np.sqrt(n_embd)
        bound2 = 1.0 / np.sqrt(d_ff)
        x = jax.random.normal(k_x, (B, S, n_embd), dtype=jnp.float32)
        W1 = jax.random.uniform(k_w1, (d_ff, n_embd), jnp.float32, -bound1, bound1)
        b1 = jax.random.uniform(k_b1, (d_ff,), jnp.float32, -bound1, bound1)
        W2 = jax.random.uniform(k_w2, (n_embd, d_ff), jnp.float32, -bound2, bound2)
        b2 = jax.random.uniform(k_b2, (n_embd,), jnp.float32, -bound2, bound2)
        return {'x': x, 'W1': W1, 'b1': b1, 'W2': W2, 'b2': b2}
    _L1_ffn_in = _L1_ffn_setup()
    _d = {'L0_attn_x': _L0_attn_in['x'], 'L0_attn_Wq': _L0_attn_in['Wq'], 'L0_attn_Wk': _L0_attn_in['Wk'], 'L0_attn_Wv': _L0_attn_in['Wv'], 'L0_attn_Wo': _L0_attn_in['Wo'], 'L0_attn_Wg': _L0_attn_in['Wg'], 'L0_attn_bg': _L0_attn_in['bg'], 'L0_ffn_router_DE': _L0_ffn_in['router_DE'], 'L0_ffn_w_in_shared_FD': _L0_ffn_in['w_in_shared_FD'], 'L0_ffn_w_out_shared_DF': _L0_ffn_in['w_out_shared_DF'], 'L0_ffn_w_swiglu_FD': _L0_ffn_in['w_swiglu_FD'], 'L0_ffn_w_in_eDF': _L0_ffn_in['w_in_eDF'], 'L0_ffn_w_swiglu_eDF': _L0_ffn_in['w_swiglu_eDF'], 'L0_ffn_w_out_eFD': _L0_ffn_in['w_out_eFD'], 'L1_attn_Wk': _L1_attn_in['Wk'], 'L1_attn_bk': _L1_attn_in['bk'], 'L1_attn_Wq': _L1_attn_in['Wq'], 'L1_attn_bq': _L1_attn_in['bq'], 'L1_attn_Wv': _L1_attn_in['Wv'], 'L1_attn_bv': _L1_attn_in['bv'], 'L1_attn_Wlr': _L1_attn_in['Wlr'], 'L1_attn_blr': _L1_attn_in['blr'], 'L1_attn_W1': _L1_attn_in['W1'], 'L1_attn_b1': _L1_attn_in['b1'], 'L1_attn_W2': _L1_attn_in['W2'], 'L1_attn_b2': _L1_attn_in['b2'], 'L1_ffn_W1': _L1_ffn_in['W1'], 'L1_ffn_b1': _L1_ffn_in['b1'], 'L1_ffn_W2': _L1_ffn_in['W2'], 'L1_ffn_b2': _L1_ffn_in['b2']}
    _x0 = _d['L0_attn_x']
    _d['L0_attn_x'] = jax.random.normal(jax.random.fold_in(jax.random.key(seed), 1), (4, 1024, 256), dtype=_x0.dtype)
    del _x0
    return _d

def reference(L0_attn_x, L0_attn_Wq, L0_attn_Wk, L0_attn_Wv, L0_attn_Wo, L0_attn_Wg, L0_attn_bg, L0_ffn_router_DE, L0_ffn_w_in_shared_FD, L0_ffn_w_out_shared_DF, L0_ffn_w_swiglu_FD, L0_ffn_w_in_eDF, L0_ffn_w_swiglu_eDF, L0_ffn_w_out_eFD, L1_attn_Wk, L1_attn_bk, L1_attn_Wq, L1_attn_bq, L1_attn_Wv, L1_attn_bv, L1_attn_Wlr, L1_attn_blr, L1_attn_W1, L1_attn_b1, L1_attn_W2, L1_attn_b2, L1_ffn_W1, L1_ffn_b1, L1_ffn_W2, L1_ffn_b2):

    def _L0_attn_ref(x, Wq, Wk, Wv, Wo, Wg, bg):
        import jax, jax.numpy as jnp
        import numpy as np
        D_MODEL = 256
        N_HEADS = 16
        D_HEAD = D_MODEL // N_HEADS
        SCALE = 1.0 / np.sqrt(D_HEAD).astype(np.float32)

        def _feature_map(x):
            return jax.nn.elu(x) + 1.0
        b, s, _ = x.shape
        q = (x @ Wq.T).reshape(b, s, N_HEADS, D_HEAD)
        k = (x @ Wk.T).reshape(b, s, N_HEADS, D_HEAD)
        v = (x @ Wv.T).reshape(b, s, N_HEADS, D_HEAD)
        q = _feature_map(q * SCALE)
        k = _feature_map(k)
        gate = jax.nn.sigmoid(x @ Wg.T + bg)
        qt = jnp.moveaxis(q, 1, 0)
        kt = jnp.moveaxis(k, 1, 0)
        vt = jnp.moveaxis(v, 1, 0)
        gt = jnp.moveaxis(gate, 1, 0)
        S0 = jnp.zeros((b, N_HEADS, D_HEAD, D_HEAD), dtype=x.dtype)

        def step(S, inp):
            q_t, k_t, v_t, g_t = inp
            S = g_t[:, :, None, None] * S + k_t[..., :, None] * v_t[..., None, :]
            y_t = jnp.einsum('bhi,bhij->bhj', q_t, S)
            return (S, y_t)
        _, ys = jax.lax.scan(step, S0, (qt, kt, vt, gt))
        y = jnp.moveaxis(ys, 0, 1).reshape(b, s, D_MODEL)
        return y @ Wo.T

    def _L0_ffn_ref(x_bsD, router_DE, w_in_shared_FD, w_out_shared_DF, w_swiglu_FD, w_in_eDF, w_swiglu_eDF, w_out_eFD):
        import jax, jax.numpy as jnp
        import numpy as np
        TOP_K = 2
        E = 8
        D = 256
        F = 512
        B, S = (2, 256)
        b, s, d = x_bsD.shape
        x_aD = x_bsD.reshape(-1, d)
        a = x_aD.shape[0]
        scores_aE = x_aD @ router_DE
        topv_aK, topi_aK = jax.lax.top_k(scores_aE, TOP_K)
        masked_aE = jnp.full_like(scores_aE, -jnp.inf)
        masked_aE = masked_aE.at[jnp.arange(a)[:, None], topi_aK].set(topv_aK)
        gates_Ea = jax.nn.sigmoid(masked_aE.astype(jnp.float32)).astype(x_aD.dtype).T
        routed_in_EaD = x_aD[None, :, :] * gates_Ea[:, :, None]
        routed_in_EaD = jax.lax.stop_gradient(routed_in_EaD)
        mid_EaF = jnp.einsum('ead,edf->eaf', routed_in_EaD, w_in_eDF)
        sw_EaF = jnp.einsum('ead,edf->eaf', routed_in_EaD, w_swiglu_eDF)
        h_EaF = jax.nn.silu(mid_EaF) * sw_EaF
        out_EaD = jnp.einsum('eaf,efd->ead', h_EaF, w_out_eFD)
        shared_aF = jax.nn.silu(x_aD @ w_in_shared_FD.T) * (x_aD @ w_swiglu_FD.T)
        shared_out_aD = jax.lax.stop_gradient(shared_aF @ w_out_shared_DF.T)
        out_aD = shared_out_aD + jnp.sum(out_EaD, axis=0)
        return out_aD.reshape(b, s, d)

    def _L1_attn_ref(x, Wk, bk, Wq, bq, Wv, bv, Wlr, blr, W1, b1, W2, b2):
        import jax, jax.numpy as jnp
        import numpy as np
        D = 256
        B, S = (4, 1024)
        LR = 0.01
        WD = 0.01
        MAX_ALR = 0.1
        EPS = 1e-08

        def _lmm(params, h):
            for W, b in params:
                h = h + jax.nn.silu(h @ W + b)
            return h

        def _reference_tuple_inner(x, Wk, bk, Wq, bq, Wv, bv, Wlr, blr, W1, b1, W2, b2):
            keys = x @ Wk + bk
            queries = x @ Wq + bq
            values = x @ Wv + bv
            alr = MAX_ALR * jax.nn.sigmoid(x @ Wlr + blr).reshape(-1)
            kf = keys.reshape(-1, D)
            vf = values.reshape(-1, D)
            params = ((W1, b1), (W2, b2))

            def loss_fn(ps):
                pred = _lmm(ps, kf)
                per_tok = jnp.mean((pred - vf) ** 2, axis=-1)
                return jnp.sum(per_tok * alr)
            grads = jax.grad(loss_fn)(params)

            def adamw(p, g):
                return p * (1.0 - LR * WD) - LR * g / (jnp.sqrt(g * g) + EPS)
            new_params = jax.tree_util.tree_map(adamw, params, grads)
            retrieved = _lmm(new_params, queries)
            surprises = jax.tree_util.tree_map(lambda g: -g, grads)
            return (retrieved, *jax.tree_util.tree_leaves(surprises))
        return _reference_tuple_inner(x, Wk, bk, Wq, bq, Wv, bv, Wlr, blr, W1, b1, W2, b2)[0]

    def _L1_ffn_ref(x, W1, b1, W2, b2):
        import jax, jax.numpy as jnp
        import numpy as np
        EPS = 1e-05

        def _quantize(W):
            gamma = jnp.mean(jnp.abs(W))
            return jnp.clip(jnp.round(W / (gamma + EPS)), -1.0, 1.0)
        Wq1 = _quantize(W1)
        Wq2 = _quantize(W2)
        h = jax.nn.relu(jnp.einsum('bsd,fd->bsf', x, Wq1) + b1)
        out = jnp.einsum('bsf,df->bsd', h, Wq2) + b2
        return out
    x = L0_attn_x
    x = _layernorm(x + _L0_attn_ref(x, L0_attn_Wq, L0_attn_Wk, L0_attn_Wv, L0_attn_Wo, L0_attn_Wg, L0_attn_bg), axis=-1)
    x = _layernorm(x + _L0_ffn_ref(x, L0_ffn_router_DE, L0_ffn_w_in_shared_FD, L0_ffn_w_out_shared_DF, L0_ffn_w_swiglu_FD, L0_ffn_w_in_eDF, L0_ffn_w_swiglu_eDF, L0_ffn_w_out_eFD), axis=-1)
    x = _layernorm(x + _L1_attn_ref(x, L1_attn_Wk, L1_attn_bk, L1_attn_Wq, L1_attn_bq, L1_attn_Wv, L1_attn_bv, L1_attn_Wlr, L1_attn_blr, L1_attn_W1, L1_attn_b1, L1_attn_W2, L1_attn_b2), axis=-1)
    x = _layernorm(x + _L1_ffn_ref(x, L1_ffn_W1, L1_ffn_b1, L1_ffn_W2, L1_ffn_b2), axis=-1)
    return x

_drawn_inputs = setup_inputs


def setup_inputs(seed=0):
    import zlib

    import numpy as np

    out = dict(_drawn_inputs(seed))
    spreads = {}
    factors = {'L0_attn_bg': 7.832,
     'L0_ffn_router_DE': 5.31,
     'L0_ffn_w_in_eDF': 4.659,
     'L0_ffn_w_swiglu_eDF': 4.657,
     'L0_ffn_w_out_eFD': 4.627,
     'L1_attn_bk': 3.211,
     'L1_attn_bv': 5.315,
     'L1_attn_Wlr': 3.648,
     'L1_attn_b1': 3.042,
     'L1_attn_b2': 3.505,
     'L1_ffn_b1': 21.526,
     'L1_ffn_b2': 64.0,
     'L0_ffn_w_in_shared_FD': 6.406,
     'L0_ffn_w_out_shared_DF': 6.363,
     'L0_ffn_w_swiglu_FD': 6.323}
    for name, (base, spread) in spreads.items():
        noise = np.random.default_rng([zlib.crc32(name.encode()), seed]).standard_normal(out[name].shape)
        drawn = base * np.exp(spread * noise) if base else spread * noise
        out[name] = jnp.asarray(drawn.astype(out[name].dtype))
    for name, factor in factors.items():
        out[name] = (out[name] * factor).astype(out[name].dtype)
    return out
```

```python
from contextlib import ExitStack

import concourse.bass as bass
from concourse import mybir

F32 = mybir.dt.float32
BF16 = mybir.dt.bfloat16
I32 = mybir.dt.int32
U32 = mybir.dt.uint32
ALU = mybir.AluOpType
ACT = mybir.ActivationFunctionType
AX = mybir.AxisListType

P = 128
B, S, D = 4, 1024, 256
NTOK = B * S
NT = NTOK // P
NC = S // P
G = D // P
H, DH = 16, 16
E8 = 8
F = 512
EPS = 1e-5
NI = 72
assert NI >= 2 * NTOK // P + E8 - 1 and NI % 4 == 0


def wait(e, sem, value):
    if isinstance(value, int) and value <= 0:
        return
    e.wait_ge(sem, value)


def wait_apart(e, mem, *waits):
    waits = [(sem, value if isinstance(value, int) else e.to_reg(value)) for sem, value in waits]
    e.wait_ge(mem["begun"], 1)
    for sem, value in waits:
        wait(e, sem, value)


def four_steps(e, lo, main_lo, main_hi, hi, body):
    for n in range(lo, main_lo):
        body(n, n % 4, n // 4)
    with e.Fori(main_lo // 4, main_hi // 4) as turn:
        for m in range(4):
            body(turn * 4 + m, m, turn)
    for n in range(main_hi, hi):
        body(n, n % 4, n // 4)


def blocks(e, count, body):
    body(0)
    with e.Fori(1, count) as q:
        body(q)


def has(n, back, count=NT):
    return not isinstance(n, int) or 0 <= n - back < count


def build_gates(nc, ctx, io, mem):
    def sem(name):
        return ctx2.enter_context(nc.semaphore(name))

    with ExitStack() as ctx2:
        def sb(name, shape, dt=F32):
            return ctx2.enter_context(nc.sbuf_tensor(name, shape, dt))

        gT = sb("g_gT", [P, S])
        d0 = sb("g_d0", [P, S])
        d1 = sb("g_d1", [P, S])
        ET = sb("g_ET", [P, S])
        part = sb("g_part", [P, 3, S], BF16)
        rest1 = sb("g_rest1", [P, S])
        rest2 = sb("g_rest2", [P, S])
        last = sb("g_last", [P, B, NC])
        WgT = sb("g_WgT", [P, G, 32])
        bg = sb("g_bg", [P, 1])
        rep = sb("g_rep", [P, G, P])
        bmask = sb("g_bmask", [P, B])
        xT = sb("g_xT", [P, G, NTOK])
        Z = ctx2.enter_context(nc.psum_tensor("g_Z", [P, 2, 512], F32))
        TP = ctx2.enter_context(nc.psum_tensor("g_TP", [P, NC, P], F32))
        DP = ctx2.enter_context(nc.psum_tensor("g_DP", [P, 512], F32))
        zeroed, wg_in, x_in, cst_in = sem("g_zeroed"), sem("g_wg_in"), [sem(f"g_x_in{b}") for b in range(B)], sem("g_cst_in")
        z_ready, g_ready, dve_step, et_ready = sem("g_z_ready"), sem("g_g_ready"), sem("g_dve_step"), sem("g_et_ready")
        parts_ready, parts_out, tp_ready, last_ready = sem("g_parts_ready"), sem("g_parts_out"), sem("g_tp_ready"), sem("g_last_ready")
        res_in, dec_ready, tp_read = sem("g_res_in"), sem("g_dec_ready"), sem("g_tp_read")

        with nc.Block() as block:
            @block.sync
            def _(sp):
                sp.wait_ge(zeroed, 2)
                sp.dma_start(WgT[:, :, 0:H], io["WgT"].rearrange("(g p) h -> p g h", p=P)).then_inc(wg_in, 16)
                for b in range(B):
                    sp.dma_start(bg[32 * b:32 * b + H, :], io["bg"].rearrange("(h o) -> h o", o=1)).then_inc(wg_in, 16)
                for b in range(B):
                    sp.dma_start(xT[:, :, b * S:(b + 1) * S],
                                 io["xT"].rearrange("(g p) t -> p g t", p=P)[:, :, b * S:(b + 1) * S]).then_inc(x_in[b], 16)
                sp.dma_start(mem["ident"][:, :], io["ident"]).then_inc(cst_in, 16)
                sp.dma_start(rep[:, :, :], io["rep"].rearrange("g p m -> p g m")).then_inc(cst_in, 16)
                sp.dma_start(bmask[:, :], io["bmask"]).then_inc(cst_in, 16)
                sp.wait_ge(parts_ready, 3)
                sp.dma_start(mem["g_parts"].rearrange("k p s -> p k s"), part[:, :, :]).then_inc(parts_out, 16)
                sp.wait_ge(parts_out, 16)
                sp.wait_ge(cst_in, 48)

            @block.tensor
            def _(pe):
                pe.wait_ge(wg_in, 16 * 5)
                for b in range(B):
                    pe.wait_ge(x_in[b], 16)
                    for half in range(2):
                        for g in range(G):
                            mm = pe.matmul(Z[32 * b:32 * b + 32, half, :], WgT[:, g, :],
                                           xT[:, g, b * S + half * 512:b * S + (half + 1) * 512],
                                           start=(g == 0), stop=(g == G - 1))
                mm.then_inc(z_ready, 1)
                pe.wait_ge(cst_in, 48)
                pe.wait_ge(et_ready, 1)
                for c in range(NC):
                    mm = pe.transpose(TP[:, c, :], ET[:, c * P:(c + 1) * P], mem["ident"][:, :])
                mm.then_inc(tp_ready, 1)
                pe.wait_ge(last_ready, B)
                for g in range(G):
                    mm = pe.matmul(DP[:, g * 32:(g + 1) * 32], rep[:, g, :], last[:, :, :].rearrange("p b c -> p (b c)"),
                                   start=True, stop=True)
                mm.then_inc(dec_ready, 1)

            @block.scalar
            def _(act):
                act.wait_ge(z_ready, 1)
                act.wait_ge(wg_in, 16 * 5)
                act.activation(gT[:, :], Z[:, :, :].rearrange("p a n -> p (a n)"), ACT.Sigmoid, bias=bg[:, 0:1]).then_inc(g_ready, 1)
                act.wait_ge(tp_ready, 1)
                act.activation(mem["Etok"][:, :, :], TP[:, :, :], ACT.Copy).then_inc(tp_read, 1)
                act.wait_ge(tp_read, 1)

            @block.vector
            def _(v):
                v.memset(bg[:, :], 0.0).then_inc(mem["begun"], 1)
                v.wait_ge(mem["begun"], 1)
                v.memset(WgT[:, :, :], 0.0).then_inc(zeroed, 1)
                v.memset(bg[:, :], 0.0).then_inc(zeroed, 1)
                v.memset(d1[:, :], 0.0).then_inc(dve_step, 1)
                v.wait_ge(g_ready, 1)
                v.wait_ge(dve_step, 1)
                v.tensor_copy(d0[:, :], gT[:, :]).then_inc(dve_step, 1)
                v.tensor_copy(d1[:, 0:S:P], gT[:, 0:S:P]).then_inc(dve_step, 1)
                v.tensor_copy(part[:, 0, :], gT[:, :]).then_inc(parts_ready, 1)
                v.wait_ge(dve_step, 3)
                v.memset(d0[:, 0:S:P], 0.0).then_inc(dve_step, 1)
                v.wait_ge(dve_step, 4)
                v.tensor_tensor_scan(ET[:, :], d0[:, :], d1[:, :], 0.0, ALU.mult, ALU.add).then_inc(et_ready, 1)
                v.wait_ge(parts_ready, 1)
                v.tensor_tensor(rest1[:, :], gT[:, :], part[:, 0, :], ALU.subtract).then_inc(dve_step, 1)
                v.wait_ge(dve_step, 5)
                v.tensor_copy(part[:, 1, :], rest1[:, :]).then_inc(parts_ready, 1)
                v.wait_ge(parts_ready, 2)
                v.tensor_tensor(rest2[:, :], rest1[:, :], part[:, 1, :], ALU.subtract).then_inc(dve_step, 1)
                v.wait_ge(dve_step, 6)
                v.tensor_copy(part[:, 2, :], rest2[:, :]).then_inc(parts_ready, 1)
                v.wait_ge(et_ready, 1)
                v.wait_ge(cst_in, 48)
                for b in range(B):
                    v.tensor_scalar(last[:, b, :], ET[:, P - 1:S:P], bmask[:, b:b + 1], None, ALU.mult).then_inc(last_ready, 1)
                v.wait_ge(dec_ready, 1)
                v.tensor_copy(mem["dec"][:, :, :], DP[:, 0:G * 32].rearrange("p (g n) -> p g n", g=G)).then_inc(dve_step, 1)
                v.wait_ge(dve_step, 7)


def build_attention(nc, ctx, io, mem):
    X, ident = mem["X"], mem["ident"]
    with ExitStack() as c2:
        def sb(name, shape, dt=F32):
            return c2.enter_context(nc.sbuf_tensor("a_" + name, shape, dt))

        def sem(name):
            return c2.enter_context(nc.semaphore("a_" + name))

        def bank(name):
            return c2.enter_context(nc.psum_tensor("a_" + name, [P, 512], F32))

        Wqk = sb("Wqk", [P, G, 2 * D])
        Wv = sb("Wv", [P, G, D])
        Wo = sb("Wo", [P, G, D])
        Wr = sb("Wr", [P, G, E8])
        hmask = sb("hmask", [P, 2])
        blk = sb("blk", [P, G, P])
        ones3 = sb("ones3", [3, P], BF16)
        xt = [sb(f"xt{p}", [P, G, P]) for p in range(2)]
        gr = [sb(f"gr{p}", [3, H * P], BF16) for p in range(2)]
        eqk = sb("eqk", [P, 2 * D])
        rqk = sb("rqk", [P, 2 * D])
        qk = [sb(f"qk{p}", [P, 2, G, P]) for p in range(2)]
        kh = [sb(f"kh{p}", [P, 2, G, P]) for p in range(2)]
        vt = [sb(f"vt{p}", [P, D]) for p in range(2)]
        dcy = [sb(f"dcy{p}", [P, H, P]) for p in range(2)]
        A = sb("A", [P, H, P])
        kw = sb("kw", [P, D])
        ye = sb("ye", [P, D])
        y = sb("y", [P, D])
        yT = sb("yT", [P, G, P])
        um = sb("um", [P, G, P])
        St = sb("St", [P, B, G, P])
        Sd = sb("Sd", [P, G, P])
        stat = sb("stat", [P, 6])
        mv = sb("mv", [P, 4, 2])
        nt = sb("nt", [P, 4])
        na = sb("na", [P, 4])
        rstd = sb("rstd", [P, 4])
        xn = [sb(f"xn{p}", [P, D]) for p in range(2)]
        xnT = sb("xnT", [P, G, P])
        bQK, bS, bZ = bank("bQK"), [bank("bS0"), bank("bS1")], [bank("bZ0"), bank("bZ1")]
        bM0, bM1, bM2 = bank("bM0"), bank("bM1"), bank("bM2")

        zero = sb("zero", [P, D])
        w_in, init, ex_in = sem("w_in"), sem("init"), sem("ex_in")
        xt_in = [sem("xt_in0"), sem("xt_in1")]
        gr_in = [sem("gr_in0"), sem("gr_in1")]
        qk_ready, qk_read, act_phi, phi_done, km_done = sem("qk_ready"), sem("qk_read"), sem("act_phi"), sem("phi_done"), sem("km_done")
        v_ready, v_read, z_ready, d_done, s_ready, a_done, av_done = (sem(k) for k in ("v_ready", "v_read", "z_ready", "d_done", "s_ready", "a_done", "av_done"))
        kt_ready, kw_done, y2_done, ye_done, y_done = (sem(k) for k in ("kt_ready", "kw_done", "y2_done", "ye_done", "y_done"))
        yt_ready, yt_read, o_ready, res_done, bn_done, ag_done = (sem(k) for k in ("yt_ready", "yt_read", "o_ready", "res_done", "bn_done", "ag_done"))
        u_ready, um_done, sd_done, st_step, nw = (sem(k) for k in ("u_ready", "um_done", "sd_done", "st_step", "newton"))
        xn_done, xnt_ready, xnt_read, xc_done, r_ready, r_read, mx_done, mi_done = (
            sem(k) for k in ("xn_done", "xnt_ready", "xnt_read", "xc_done", "r_ready", "r_read", "mx_done", "mi_done"))
        NWT = 12

        LO, ML, MH, HI = 0, 8, NT, NT + 7
        QK_READS = 2

        with nc.Block() as block:
            @block.sync
            def _(sp):
                for dst, name in ((Wv, "WvT"), (Wo, "WoT"), (Wr, "router")):
                    sp.dma_start(dst[:, :, :], io[name].rearrange("(g p) n -> p g n", p=P)).then_inc(w_in, 16)
                sp.dma_start(Wqk[:, :, 0:D], io["WqT"].rearrange("(g p) n -> p g n", p=P)).then_inc(w_in, 16)
                sp.dma_start(Wqk[:, :, D:2 * D], io["WkT"].rearrange("(g p) n -> p g n", p=P)).then_inc(w_in, 16)
                sp.dma_start(hmask[:, :], io["hmask"]).then_inc(w_in, 16)
                sp.dma_start(blk[:, :, :], io["blk"].rearrange("g p n -> p g n")).then_inc(w_in, 16)
                sp.dma_start(X[:, :, :].rearrange("p (c b) d -> p c b d", b=B)[:, :, 0, :],
                             io["x"][0].rearrange("(c p) d -> p c d", p=P)).then_inc(w_in, 16)
                for b in range(1, B):
                    sp.dma_start(X[:, :, :].rearrange("p (c b) d -> p c b d", b=B)[:, :, b, :],
                                 io["x"][b].rearrange("(c p) d -> p c d", p=P)).then_inc(w_in, 16)

                def body(n, m, turn):
                    if not has(n, 0):
                        return
                    p = m % 2
                    wait(sp, v_ready, n - 1)
                    sp.dma_start(xt[p][:, :, :], io["xT"].rearrange("(g p) (b t) -> p g b t", p=P, b=B)[:, :, m, bass.ds(turn * P, P)]).then_inc(xt_in[p], 16)
                    wait_apart(sp, mem, (z_ready, 4 * (n - 1)))
                    sp.dma_start(gr[p][:, :].rearrange("k (h t) -> k h t", h=H),
                                 mem["g_parts"][:, 32 * m:32 * m + H, bass.ds(turn * P, P)]).then_inc(gr_in[p], 16)

                four_steps(sp, LO, ML, MH, NT, body)
                for e in range(E8 + 1):
                    for dst, src in ((mem["Win"], io["w_in"]), (mem["Wsw"], io["w_sw"])):
                        sp.dma_start(dst[:, e, :, :], src[e].rearrange("(g p) f -> p g f", p=P)).then_inc(ex_in, 16)
                sp.wait_ge(init, 3)
                for k in range(8):
                    r = NI * P // 8
                    sp.dma_start(mem["rows"][k * r:(k + 1) * r, :].rearrange("(a p) d -> p a d", p=P),
                                 zero[:, :].unsqueeze(1).to_broadcast([P, r // P, D])).then_inc(ex_in, 16)
                sp.wait_ge(ex_in, 16 * (2 * (E8 + 1) + 8))

            def run(e, body):
                four_steps(e, LO, ML, MH, HI, body)

            @block.tensor
            def _(pe):
                pe.wait_ge(w_in, 16 * 11)
                pe.wait_ge(init, 3)

                def gates(n, m, turn, r):
                    if r == 0:
                        pe.wait_ge(gr_in[m % 2], 16 * (2 * turn + m // 2 + 1))
                    wait(pe, d_done, 4 * n + r - 1)
                    pe.matmul(bZ[r % 2][:, :], ones3[:, :], gr[m % 2][:, r * 512:(r + 1) * 512],
                              start=True, stop=True).then_inc(z_ready, 1)

                def scores(i, m, r):
                    p = (m - 1) % 2
                    if r == 0:
                        pe.wait_ge(phi_done, i + 1)
                        pe.wait_ge(km_done, i + 1)
                    wait(pe, a_done, 4 * i + r - 1)
                    for g in range(G):
                        for e in range(2):
                            mm = pe.matmul(bS[r % 2][:, (2 * g + e) * P:(2 * g + e + 1) * P],
                                           kh[p][32 * r:32 * r + 32, e, g, :], qk[p][32 * r:32 * r + 32, 0, g, :],
                                           start=True, stop=True)
                    mm.then_inc(s_ready, 1)

                def values(i, m, r):
                    p = (m - 1) % 2
                    if r == 0:
                        pe.wait_ge(v_read, i + 1)
                    pe.wait_ge(a_done, 4 * i + r + 1)
                    for j in range(4 * r, 4 * r + 4):
                        mm = pe.matmul(bM1[:, D + j * DH:D + (j + 1) * DH], A[:, j, :], vt[p][:, j * DH:(j + 1) * DH],
                                       start=True, stop=True)
                    mm.then_inc(av_done, 1)

                def body(n, m, turn):
                    i, p1 = n - 1, (m - 1) % 2
                    if has(n, 0):
                        p = m % 2
                        pe.wait_ge(xt_in[p], 16 * (2 * turn + m // 2 + 1))
                        wait(pe, qk_read, QK_READS * n)
                        for o in range(4):
                            for g in range(G):
                                mm = pe.matmul(bQK[:, o * P:(o + 1) * P], Wqk[:, g, o * P:(o + 1) * P], xt[p][:, g, :],
                                               start=(g == 0), stop=(g == G - 1))
                        mm.then_inc(qk_ready, 1)
                        if has(n, 7):
                            wait(pe, xnt_read, n - 6)
                        elif has(n, 3):
                            wait(pe, yt_read, n - 2)
                        else:
                            wait(pe, v_read, n)
                        for g in range(G):
                            mm = pe.matmul(bM0[:, 0:D], xt[p][:, g, :], Wv[:, g, :], start=(g == 0), stop=(g == G - 1))
                        mm.then_inc(v_ready, 1)
                    if has(n, 1):
                        scores(i, m, 0)
                    if has(n, 0):
                        gates(n, m, turn, 0)
                    if has(n, 1):
                        wait(pe, y_done, i)
                        for g in range(G):
                            mm = pe.transpose(bM1[:, g * P:(g + 1) * P], qk[p1][:, 1, g, :], ident[:, :])
                        mm.then_inc(kt_ready, 1)
                    if has(n, 2):
                        j = n - 2
                        if has(n, 0):
                            pe.wait_ge(v_read, n + 1)
                        pe.wait_ge(y_done, j + 1)
                        if not has(n, 0) and has(n, 7):
                            wait(pe, xnt_read, n - 6)
                        for g in range(G):
                            mm = pe.transpose(bM0[:, g * P:(g + 1) * P], y[:, g * P:(g + 1) * P], ident[:, :])
                        mm.then_inc(yt_ready, 1)
                    if has(n, 1):
                        scores(i, m, 1)
                    if has(n, 0):
                        gates(n, m, turn, 1)
                    if has(n, 1):
                        pe.wait_ge(kw_done, 2 * (i + 1))
                        wait(pe, st_step, 2 * (i - 3))
                        yv = bM1[:, 0:D].rearrange("p (r g c) -> p g r c", r=4, g=G)
                        for g in range(G):
                            mm = pe.matmul(yv[:, g], qk[p1][:, 0, g, :],
                                           St[:, (m - 1) % 4, g, :].rearrange("p (r c) -> p r c", r=4), start=True, stop=True)
                        mm.then_inc(y2_done, 1)
                        values(i, m, 0)
                    if has(n, 2):
                        wait(pe, um_done, n - 1)
                        if has(n, 7):
                            wait(pe, r_read, n - 6)
                        pe.wait_ge(yt_read, n - 1)
                        for g in range(G):
                            mm = pe.matmul(bM2[:, 0:D], yT[:, g, :], Wo[:, g, :], start=(g == 0), stop=(g == G - 1))
                        mm.then_inc(o_ready, 1)
                    if has(n, 6):
                        pe.wait_ge(xn_done, n - 5)
                        if has(n, 2):
                            pe.wait_ge(yt_read, n - 1)
                        else:
                            wait(pe, xnt_read, n - 6)
                        for g in range(G):
                            mm = pe.transpose(bM0[:, g * P:(g + 1) * P], xn[m % 2][:, g * P:(g + 1) * P], ident[:, :])
                        mm.then_inc(xnt_ready, 1)
                    for r in (2, 3):
                        if has(n, 1):
                            scores(i, m, r)
                        if has(n, 0):
                            gates(n, m, turn, r)
                        if has(n, 1):
                            values(i, m, r - 1)
                    if has(n, 1):
                        values(i, m, 3)
                    if has(n, 2):
                        pe.wait_ge(res_done, n - 1)
                    if has(n, 1):
                        for g in range(G):
                            mm = pe.matmul(bM2[:, g * P:(g + 1) * P], kw[:, g * P:(g + 1) * P],
                                           vt[p1][:, :].rearrange("p (r g c) -> p g r c", r=4, g=G)[:, g], start=True, stop=True)
                        mm.then_inc(u_ready, 1)
                    if has(n, 6):
                        pe.wait_ge(xnt_read, n - 5)
                        if not has(n, 2):
                            wait(pe, r_read, n - 6)
                        for g in range(G):
                            mm = pe.matmul(bM2[:, D:D + E8], xnT[:, g, :], Wr[:, g, :], start=(g == 0), stop=(g == G - 1))
                        mm.then_inc(r_ready, 1)

                run(pe, body)

            @block.scalar
            def _(act):
                def body(n, m, turn):
                    if has(n, 0):
                        act.wait_ge(qk_ready, n + 1)
                        wait(act, phi_done, n)
                        act.activation(eqk[:, 0:D], bQK[:, 0:D], ACT.Exp, scale=0.25).then_inc(act_phi, 1)
                        act.activation(eqk[:, D:2 * D], bQK[:, D:2 * D], ACT.Exp).then_inc(act_phi, 1)
                        act.activation(rqk[:, 0:D], bQK[:, 0:D], ACT.Relu, scale=0.25).then_inc(qk_read, 1)
                        act.activation(rqk[:, D:2 * D], bQK[:, D:2 * D], ACT.Relu).then_inc(qk_read, 1)
                        act.wait_ge(v_ready, n + 1)
                        wait(act, u_ready, n - 1)
                        act.activation(vt[m % 2][:, :], bM0[:, 0:D], ACT.Copy).then_inc(v_read, 1)
                    if has(n, 2):
                        act.wait_ge(yt_ready, n - 1)
                        wait(act, o_ready, n - 2)
                        act.activation(yT[:, :, :].rearrange("p g t -> p (g t)"), bM0[:, 0:D], ACT.Copy).then_inc(yt_read, 1)
                    if has(n, 6):
                        act.wait_ge(xnt_ready, n - 5)
                        wait(act, r_ready, n - 6)
                        act.activation(xnT[:, :, :].rearrange("p g t -> p (g t)"), bM0[:, 0:D], ACT.Copy).then_inc(xnt_read, 1)

                run(act, body)

            @block.vector
            def _(v):
                v.memset(ones3[:, :], 1.0).then_inc(init, 1)
                v.memset(St[:, :, :, :], 0.0).then_inc(init, 1)
                v.memset(zero[:, :], 0.0).then_inc(init, 1)
                v.wait_ge(w_in, 16 * 11)

                def weigh(i, m, r):
                    v.wait_ge(s_ready, 4 * i + r + 1)
                    wait(v, av_done, 4 * (i - 1) + r + 1)
                    v.wait_ge(d_done, 4 * i + r + 1)
                    v.tensor_tensor(A[:, 4 * r:4 * r + 4, :], bS[r % 2][:, :].rearrange("p (h t) -> p h t", h=4),
                                    dcy[(m - 1) % 2][:, 4 * r:4 * r + 4, :], ALU.mult).then_inc(a_done, 1)

                def decay(n, m, r):
                    v.wait_ge(z_ready, 4 * n + r + 1)
                    wait(v, a_done, 4 * (n - 2) + r + 1)
                    wait(v, kw_done, 2 * (n - 1))
                    for h in range(4):
                        ins = v.tensor_tensor_scan(dcy[m % 2][:, 4 * r + h, :], bZ[r % 2][:, h * P:(h + 1) * P], ident[:, :],
                                                   0.0, ALU.mult, ALU.add)
                    ins.then_inc(d_done, 1)

                def body(n, m, turn):
                    i = n - 1
                    if has(n, 2):
                        j = n - 2
                        cj = turn if m >= 2 else turn - 1
                        bj = (m - 2) % 4
                        v.wait_ge(av_done, 4 * (j + 1))
                        v.wait_ge(y2_done, j + 1)
                        v.tensor_tensor(ye[:, :].rearrange("p (h c) -> p h c", h=H), bM1[:, 0:D].rearrange("p (h c) -> p h c", h=H),
                                        mem["Etok"][:, bass.ds(cj, 1), 32 * bj:32 * bj + H].rearrange("p o h -> p (o h)").unsqueeze(2).to_broadcast([P, H, DH]),
                                        ALU.mult).then_inc(ye_done, 1)
                        v.wait_ge(ye_done, j + 1)
                        wait(v, yt_ready, j)
                        v.tensor_tensor(y[:, :], bM1[:, D:2 * D], ye[:, :], ALU.add).then_inc(y_done, 1)
                        v.wait_ge(u_ready, j + 1)
                        if has(n, 7):
                            v.wait_ge(r_ready, n - 6)
                        wait(v, st_step, 2 * j)
                        v.tensor_tensor(um[:, :, :], bM2[:, 0:D].rearrange("p (g c) -> p g c", g=G), blk[:, :, :], ALU.mult).then_inc(um_done, 1)
                    if has(n, 7):
                        t = n - 7
                        v.wait_ge(r_ready, t + 1)
                        v.tensor_copy(mem["score"][:, bass.ds(t, 1), :].rearrange("p o e -> p (o e)"), bM2[:, D:D + E8]).then_inc(r_read, 1)
                    if has(n, 6):
                        t, q = n - 6, (m - 6) % 4
                        grp = turn - 1 if m >= 2 else turn - 2
                        v.wait_ge(nw, NWT * (grp + 1))
                        wait(v, xnt_ready, t - 1)
                        wait(v, xc_done, t - 1)
                        v.tensor_scalar(xn[m % 2][:, :], X[:, bass.ds(t, 1), :].rearrange("p o d -> p (o d)"), mv[:, q, 0:1], rstd[:, q:q + 1],
                                        ALU.subtract, ALU.mult).then_inc(xn_done, 1)
                    if has(n, 1):
                        weigh(i, m, 0)
                    if has(n, 0):
                        decay(n, m, 0)
                    if has(n, 1):
                        v.wait_ge(kt_ready, i + 1)
                        wait(v, u_ready, i)
                        v.wait_ge(d_done, 4 * i + 4)
                        dl = dcy[(m - 1) % 2][:, :, P - 1:P].rearrange("p (r g e) o -> p g r (e o)", r=4, g=G)
                        for g in range(G):
                            v.tensor_tensor(kw[:, g * P:(g + 1) * P].rearrange("p (r e c) -> p r e c", r=4, e=2),
                                            bM1[:, g * P:(g + 1) * P].rearrange("p (r e c) -> p r e c", r=4, e=2),
                                            dl[:, g].unsqueeze(3).to_broadcast([P, 4, 2, DH]), ALU.mult).then_inc(kw_done, 1)
                    for r in (1, 2, 3):
                        if has(n, 1):
                            weigh(i, m, r)
                        if has(n, 0):
                            decay(n, m, r)
                        if r == 2 and has(n, 0):
                            v.wait_ge(act_phi, 2 * (n + 1))
                            v.wait_ge(qk_read, QK_READS * (n + 1))
                            wait(v, u_ready, n - 1)
                            wait(v, km_done, n - 1)
                            v.scalar_tensor_tensor(out=qk[m % 2][:, :, :, :].rearrange("p a g t -> p (a g t)"), in0=eqk[:, :], scalar=1.0,
                                                   in1=rqk[:, :], op0=ALU.min, op1=ALU.add).then_inc(phi_done, 1)
                    if has(n, 2):
                        j, q = n - 2, (m - 2) % 4
                        xj = X[:, bass.ds(j, 1), :].rearrange("p o d -> p (o d)")
                        v.wait_ge(o_ready, j + 1)
                        v.tensor_tensor(xj, bM2[:, 0:D], xj, ALU.add).then_inc(res_done, 1)
                        wait_apart(v, mem, (res_done, j + 1), (ag_done, j))
                        v.bn_stats(stat[:, :], xj).then_inc(bn_done, 1)
                        wait_apart(v, mem, (bn_done, j + 1), (xn_done, j - 3))
                        v.bn_aggr(mv[:, q, :], stat[:, :]).then_inc(ag_done, 1)
                        if q == 3:
                            grp = turn - 1
                            v.wait_ge(ag_done, j + 1)
                            rsqrt_group(v, nw, NWT * grp, mv[:, :, 1], nt[:, :], na[:, :], rstd[:, :])

                run(v, body)
                v.wait_ge(r_read, NT)
                for t in range(NT):
                    v.max(mem["topv"][:, t, :], mem["score"][:, t, :]).then_inc(mx_done, 1)
                for t in range(NT):
                    v.wait_ge(mx_done, t + 1)
                    v.max_index(mem["topi"][:, t, :], mem["topv"][:, t, :], mem["score"][:, t, :]).then_inc(mi_done, 1)
                v.wait_ge(mi_done, NT)

            @block.gpsimd
            def _(pool):
                pool.wait_ge(w_in, 16 * 11)
                pool.wait_ge(init, 3)

                def body(n, m, turn):
                    if has(n, 2):
                        j, bj = n - 2, (m - 2) % 4
                        ti = turn if m >= 2 else turn - 1
                        wait_apart(pool, mem, (st_step, 2 * j))
                        pool.tensor_tensor(Sd[:, :, :], St[:, bj, :, :],
                                           mem["dec"][:, :, bass.ds(ti + bj * NC, 1)].to_broadcast([P, G, P]), ALU.mult).then_inc(sd_done, 1)
                        pool.wait_ge(um_done, j + 1)
                        pool.wait_ge(y2_done, j + 1)
                        pool.wait_ge(sd_done, j + 1)
                        pool.tensor_tensor(St[:, bj, :, :], Sd[:, :, :], um[:, :, :], ALU.add).then_inc(st_step, 2)
                    if has(n, 0):
                        wait_apart(pool, mem, (s_ready, 4 * (n - 1)), (phi_done, n + 1))
                        for e in range(2):
                            ins = pool.tensor_scalar(kh[m % 2][:, e, :, :], qk[m % 2][:, 1, :, :], hmask[:, e:e + 1], None, ALU.mult)
                        ins.then_inc(km_done, 1)
                    if has(n, 6):
                        t = n - 6
                        pool.wait_ge(xn_done, t + 1)
                        pool.tensor_copy(X[:, bass.ds(t, 1), :].rearrange("p o d -> p (o d)"), xn[m % 2][:, :]).then_inc(xc_done, 1)

                run(pool, body)
                pool.wait_ge(xc_done, NT)


def build_shared_and_routes(nc, io, mem):
    X = mem["X"]
    with ExitStack() as c2:
        def sb(name, shape, dt=F32):
            return c2.enter_context(nc.sbuf_tensor("r_" + name, shape, dt))

        def sem(name):
            return c2.enter_context(nc.semaphore("r_" + name))

        iota8 = sb("iota8", [P, E8])
        item = sb("item", [P, NI])
        tri = sb("tri", [P, P])
        ones = sb("ones", [P, P])
        ones8 = sb("ones8", [P, NT])
        idx_f = [sb(f"idx_f{k}", [P, NT]) for k in range(2)]
        pick = [sb(f"pick{k}", [P, NT, E8]) for k in range(2)]
        both = sb("both", [P, NT, E8])
        total = sb("total", [P, NT, E8])
        incl = sb("incl", [P, NT, E8])
        off = sb("off", [P, NT, E8])
        tmp = sb("tmp", [P, NT, E8])
        slot_f = sb("slot_f", [P, NT])
        cnt = sb("cnt", [P, E8])
        cnt_i = sb("cnt_i", [P, E8], I32)
        cnt_s = sb("cnt_s", [P, E8], I32)
        tiles = sb("tiles", [P, E8])
        ends = sb("ends", [P, E8])
        base = sb("base", [P, E8])
        cmp = sb("cmp", [1, NI, E8])
        exf = sb("exf", [1, NI])
        gate = sb("gate", [P, NT, 2])
        row = [[sb(f"row{p}{k}", [P, D]) for k in range(2)] for p in range(2)]
        rix = [[sb(f"rix{p}{k}", [P, 1], U32) for k in range(2)] for p in range(2)]
        bR = c2.enter_context(nc.psum_tensor("r_bR", [P, 2, 512], F32))

        w_in, dve, counted, gate_ready, cuts, gate_in = sem("w_in"), sem("dve"), sem("counted"), sem("gate_ready"), sem("cuts"), sem("gate_in")
        wo_in = [sem("wo_in"), sem("wo_sh_in")]
        row_ready, rix_ready = sem("row_ready"), sem("rix_ready")
        sent = [[sem(f"sent{p}{k}") for k in range(2)] for p in range(2)]

        def route(v):
            n = 0

            def link(ins):
                nonlocal n
                n += 1
                ins.then_inc(dve, 1)
                v.wait_ge(dve, n)

            v.wait_ge(w_in, 16 * 3)
            v.memset(ones[:, :], 1.0).then_inc(cuts, 1)
            link(v.memset(ones8[:, :], 1.0))
            for k in range(2):
                link(v.tensor_copy(idx_f[k][:, :], mem["topi"][:, :, k]))
                link(v.tensor_tensor(pick[k][:, :, :], iota8[:, :].unsqueeze(1).to_broadcast([P, NT, E8]),
                                     idx_f[k][:, :].unsqueeze(2).to_broadcast([P, NT, E8]), ALU.is_equal))
            v.tensor_tensor(both[:, :, :], pick[0][:, :, :], pick[1][:, :, :], ALU.add).then_inc(cuts, 1)
            v.wait_ge(counted, 1)
            link(v.tensor_copy(total[:, :, :], bR[:, 1, 0:NT * E8].rearrange("p (t e) -> p t e", e=E8)))
            for e in range(E8):
                link(v.tensor_tensor_scan(incl[:, :, e], ones8[:, :], total[:, :, e], 0.0, ALU.mult, ALU.add))
            link(v.tensor_scalar(cnt[:, :], incl[:, NT - 1, :], float(P - 1), None, ALU.add))
            link(v.tensor_copy(cnt_i[:, :], cnt[:, :]))
            link(v.tensor_scalar(cnt_s[:, :], cnt_i[:, :], 7, None, ALU.arith_shift_right))
            link(v.tensor_copy(tiles[:, :], cnt_s[:, :]))
            link(v.tensor_tensor_scan(ends[:, :], ones8[:, 0:E8], tiles[:, :], 0.0, ALU.mult, ALU.add))
            link(v.tensor_tensor(base[:, :], ends[:, :], tiles[:, :], ALU.subtract))
            link(v.tensor_scalar(base[:, :], base[:, :], float(P), None, ALU.mult))
            link(v.tensor_tensor(off[:, :, :], incl[:, :, :], total[:, :, :], ALU.subtract))
            link(v.tensor_tensor(off[:, :, :], off[:, :, :], bR[:, 0, 0:NT * E8].rearrange("p (t e) -> p t e", e=E8), ALU.add))
            link(v.tensor_tensor(off[:, :, :], off[:, :, :], base[:, :].unsqueeze(1).to_broadcast([P, NT, E8]), ALU.add))
            for k in range(2):
                link(v.tensor_tensor(tmp[:, :, :], pick[k][:, :, :], off[:, :, :], ALU.mult))
                link(v.tensor_reduce(slot_f[:, :], tmp[:, :, :], AX.X, ALU.add))
                link(v.tensor_copy(mem["slot"][:, k, :], slot_f[:, :]))
            link(v.tensor_tensor(cmp[:, :, :], item[0:1, :].unsqueeze(2).to_broadcast([1, NI, E8]),
                                 ends[0:1, :].unsqueeze(1).to_broadcast([1, NI, E8]), ALU.is_ge))
            link(v.tensor_reduce(exf[:, :], cmp[:, :, :], AX.X, ALU.add))
            link(v.tensor_scalar(exf[:, :], exf[:, :], float(E8 - 1), None, ALU.min))
            link(v.tensor_copy(mem["expert"][:, :], exf[:, :]))
            v.wait_ge(gate_ready, 1)

        def count(pe):
            pe.wait_ge(w_in, 16 * 3)
            pe.wait_ge(cuts, 2)
            pe.wait_ge(wo_in[1], 16)
            pe.matmul(bR[:, 0, 0:NT * E8], tri[:, :], both[:, :, :].rearrange("p t e -> p (t e)"), start=True, stop=True)
            pe.matmul(bR[:, 1, 0:NT * E8], ones[:, :], both[:, :, :].rearrange("p t e -> p (t e)"), start=True, stop=True).then_inc(counted, 1)

        def gates(act):
            act.activation(gate[:, :, :], mem["topv"][:, :, 0:2], ACT.Sigmoid).then_inc(gate_ready, 1)

        def dispatch_rows(v, t, m, turn):
            p = m % 2
            for k in range(2):
                if not (isinstance(t, int) and t < 2):
                    v.wait_ge(sent[p][k], 16 * (2 * turn + m // 2))
                v.tensor_scalar(row[p][k][:, :], X[:, bass.ds(t, 1), :].rearrange("p o d -> p (o d)"), gate[:, bass.ds(t, 1), k], None,
                                ALU.mult).then_inc(row_ready, 1)
                v.tensor_copy(rix[p][k][:, :], mem["slot"][:, k, bass.ds(t, 1)]).then_inc(rix_ready, 1)

        def dispatch_send(pool, t, m, turn):
            p = m % 2
            wait_apart(pool, mem, (row_ready, 2 * (t + 1)), (rix_ready, 2 * (t + 1)))
            for k in range(2):
                pool.indirect_dma_start(out=mem["rows"], out_offset=bass.IndirectOffsetOnAxis(ap=rix[p][k][:, 0:1], axis=0),
                                        in_=row[p][k][:, :], in_offset=None).then_inc(sent[p][k], 16)

        def dispatch_end(pool):
            for p in range(2):
                for k in range(2):
                    pool.wait_ge(sent[p][k], 16 * NT // 2)

        def consts(sp):
            for dst, name in ((iota8, "iota8"), (item, "item"), (tri, "tri")):
                sp.dma_start(dst[:, :], io[name]).then_inc(w_in, 16)
            for e in range(E8, -1, -1):
                sp.dma_start(mem["Wout"][:, e, :, :], io["w_out"][e].rearrange("(g p) f -> p g f", p=P)).then_inc(wo_in[e == E8], 16)

        def out_weights(sp):
            sp.wait_ge(wo_in[0], 16 * E8)

        build_expert_tiles(nc, mem, "sh_", NT, shared=True, before={"sp": consts, "act": gates, "pe": count, "v": route},
                           each={"v": dispatch_rows, "pool": dispatch_send}, after={"pool": dispatch_end, "sp": out_weights})


def build_expert_tiles(nc, mem, name_, count, shared, before={}, each={}, after={}):
    X, ident, Win, Wsw, Wout = mem["X"], mem["ident"], mem["Win"], mem["Wsw"], mem["Wout"]
    with ExitStack() as c2:
        def sb(name, shape, dt=F32):
            return c2.enter_context(nc.sbuf_tensor(name_ + name, shape, dt))

        def sem(name):
            return c2.enter_context(nc.semaphore(name_ + name))

        def bank(name):
            return c2.enter_context(nc.psum_tensor(name_ + name, [P, 512], F32))

        xg = [sb(f"xg{p}", [P, D]) for p in range(2)]
        xT = [sb(f"xT{p}", [P, G, P]) for p in range(2)]
        sl = sb("sl", [P, F])
        h = sb("h", [P, F])
        hT = sb("hT", [P, F])
        yo = [sb(f"yo{p}", [P, D]) for p in range(2)]
        bX, bA, bB, bH, bO = bank("bX"), bank("bA"), bank("bB"), bank("bH"), bank("bO")
        x_in, y_out = [sem("x_in0"), sem("x_in1")], [sem("y_out0"), sem("y_out1")]
        xt_ready, xt_read, mid_ready, sw_ready, silu_done, h_done, ht_ready, ht_read, o_ready, o_read = (
            sem(k) for k in ("xt_ready", "xt_read", "mid_ready", "sw_ready", "silu_done", "h_done", "ht_ready", "ht_read", "o_ready", "o_read"))

        def run(e, body):
            four_steps(e, 0, 4, count, count + 2, body)

        def has_(n, back):
            return has(n, back, count)

        with nc.Block() as block:
            @block.sync
            def _(sp):
                if "sp" in before:
                    before["sp"](sp)

                def body(n, m, turn):
                    if has_(n, 0):
                        p = m % 2
                        wait(sp, xt_ready, n - 1)
                        src = X[:, bass.ds(n, 1), :].rearrange("p o d -> p (o d)") if shared else mem["rows"][bass.ds(n * P, P), :]
                        sp.dma_start(xg[p][:, :], src).then_inc(x_in[p], 16)
                    if has_(n, 2) and not shared:
                        sp.wait_ge(o_read, n - 1)
                        sp.dma_start(mem["outs"][bass.ds((n - 2) * P, P), :], yo[m % 2][:, :]).then_inc(y_out[m % 2], 16)

                run(sp, body)
                if "sp" in after:
                    after["sp"](sp)
                if not shared:
                    for p in range(2):
                        sp.wait_ge(y_out[p], 16 * (count // 2))

            @block.tensor
            def _(pe):
                if "pe" in before:
                    before["pe"](pe)

                def body(n, m, turn):
                    if has_(n, 2):
                        pe.wait_ge(h_done, n - 1)
                        wait(pe, ht_read, n - 2)
                        for j in range(4):
                            mm = pe.transpose(bH[:, j * P:(j + 1) * P], h[:, j * P:(j + 1) * P], ident[:, :])
                        mm.then_inc(ht_ready, 1)
                    if has_(n, 0):
                        pe.wait_ge(x_in[m % 2], 16 * (2 * turn + m // 2 + 1))
                        wait(pe, xt_read, n)
                        for g in range(G):
                            mm = pe.transpose(bX[:, g * P:(g + 1) * P], xg[m % 2][:, g * P:(g + 1) * P], ident[:, :])
                        mm.then_inc(xt_ready, 1)
                    if has_(n, 1):
                        p = (m - 1) % 2
                        e = E8 if shared else pe.value_load(mem["expert"][0:1, bass.ds(n - 1, 1)], min_val=0, max_val=E8 - 1)
                        pe.wait_ge(xt_read, n)
                        wait(pe, silu_done, n - 1)
                        for g in range(G):
                            mm = pe.matmul(bA[:, :], xT[p][:, g, :], Win[:, bass.ds(e, 1), g, :].rearrange("p o f -> p (o f)"),
                                           start=(g == 0), stop=(g == G - 1))
                        mm.then_inc(mid_ready, 1)
                        wait(pe, h_done, n - 1)
                        for g in range(G):
                            mm = pe.matmul(bB[:, :], xT[p][:, g, :], Wsw[:, bass.ds(e, 1), g, :].rearrange("p o f -> p (o f)"),
                                           start=(g == 0), stop=(g == G - 1))
                        mm.then_inc(sw_ready, 1)
                    if has_(n, 2):
                        e = E8 if shared else pe.value_load(mem["expert"][0:1, bass.ds(n - 2, 1)], min_val=0, max_val=E8 - 1)
                        pe.wait_ge(ht_read, n - 1)
                        wait(pe, o_read, n - 2)
                        for j in range(4):
                            mm = pe.matmul(bO[:, 0:D], hT[:, j * P:(j + 1) * P], Wout[:, bass.ds(e, 1), j, :].rearrange("p o f -> p (o f)"),
                                           start=(j == 0), stop=(j == 3))
                        mm.then_inc(o_ready, 1)

                run(pe, body)

            @block.scalar
            def _(act):
                if "act" in before:
                    before["act"](act)

                def body(n, m, turn):
                    if has_(n, 0):
                        act.wait_ge(xt_ready, n + 1)
                        wait(act, sw_ready, n - 1)
                        act.activation(xT[m % 2][:, :, :].rearrange("p g t -> p (g t)"), bX[:, 0:D], ACT.Copy).then_inc(xt_read, 1)
                    if has_(n, 1):
                        act.wait_ge(mid_ready, n)
                        wait(act, h_done, n - 1)
                        act.activation(sl[:, :], bA[:, :], ACT.Silu).then_inc(silu_done, 1)
                    if has_(n, 2) and not shared:
                        act.wait_ge(o_ready, n - 1)
                        if not (isinstance(n, int) and n < 4):
                            act.wait_ge(y_out[m % 2], 16 * (2 * turn + m // 2 - 1))
                        act.activation(yo[m % 2][:, :], bO[:, 0:D], ACT.Copy).then_inc(o_read, 1)

                run(act, body)

            @block.vector
            def _(v):
                if "v" in before:
                    before["v"](v)

                def body(n, m, turn):
                    if has_(n, 2):
                        v.wait_ge(ht_ready, n - 1)
                        wait(v, o_ready, n - 2)
                        v.tensor_copy(hT[:, :], bH[:, :]).then_inc(ht_read, 1)
                    if has_(n, 0) and "v" in each:
                        each["v"](v, n, m, turn)
                    if has_(n, 1):
                        v.wait_ge(silu_done, n)
                        v.wait_ge(sw_ready, n)
                        wait(v, ht_ready, n - 1)
                        v.tensor_tensor(h[:, :], bB[:, :], sl[:, :], ALU.mult).then_inc(h_done, 1)
                    if has_(n, 2) and shared:
                        v.wait_ge(o_ready, n - 1)
                        xj = X[:, bass.ds(n - 2, 1), :].rearrange("p o d -> p (o d)")
                        v.tensor_tensor(xj, bO[:, 0:D], xj, ALU.add).then_inc(o_read, 1)

                run(v, body)
                if shared:
                    v.wait_ge(o_read, count)

            @block.gpsimd
            def _(pool):
                if "pool" in each:
                    four_steps(pool, 0, 4, count, count, lambda n, m, turn: each["pool"](pool, n, m, turn))
                if "pool" in after:
                    after["pool"](pool)


def build_combine(nc, mem):
    X = mem["X"]
    with ExitStack() as c2:
        def sb(name, shape, dt=F32):
            return c2.enter_context(nc.sbuf_tensor("c_" + name, shape, dt))

        def sem(name):
            return c2.enter_context(nc.semaphore("c_" + name))

        XT, ident = mem["XT"], mem["ident"]
        xs = [sb(f"xs{q}", [P, D]) for q in range(4)]
        bT = [c2.enter_context(nc.psum_tensor(f"c_bT{g}", [P, 512], F32)) for g in range(G)]
        xc_done, xt_ready, xt_read = sem("xc_done"), sem("xt_ready"), sem("xt_read")
        gix = [[sb(f"gix{p}{k}", [P, 1], U32) for k in range(2)] for p in range(2)]
        got = [[sb(f"got{p}{k}", [P, D]) for k in range(2)] for p in range(2)]
        stat, mv = sb("stat", [P, 6]), sb("mv", [P, 4, 2])
        nt, na, rstd = sb("nt", [P, 4]), sb("na", [P, 4]), sb("rstd", [P, 4])
        gix_ready, add1, add2, bn_done, ag_done, nw, xn_done = (sem(k) for k in ("gix_ready", "add1", "add2", "bn_done", "ag_done", "nw", "xn_done"))
        came = [[sem(f"came{p}{k}") for k in range(2)] for p in range(2)]

        with nc.Block() as block:
            @block.vector
            def _(v):
                def body(n, m, turn):
                    p = m % 2
                    if has(n, 0):
                        for k in range(2):
                            if not (isinstance(n, int) and n < 2):
                                v.wait_ge(came[p][k], 16 * (2 * turn + m // 2))
                            v.tensor_copy(gix[p][k][:, :], mem["slot"][:, k, bass.ds(n, 1)]).then_inc(gix_ready, 1)
                    if has(n, 1):
                        j, q = n - 1, (m - 1) % 4
                        xj = X[:, bass.ds(j, 1), :].rearrange("p o d -> p (o d)")
                        fills = 2 * turn + m // 2 + (m % 2)
                        v.wait_ge(came[q % 2][0], 16 * fills)
                        v.tensor_tensor(xj, xj, got[q % 2][0][:, :], ALU.add).then_inc(add1, 1)
                        v.wait_ge(add1, j + 1)
                        v.wait_ge(came[q % 2][1], 16 * fills)
                        v.tensor_tensor(xj, xj, got[q % 2][1][:, :], ALU.add).then_inc(add2, 1)
                        wait_apart(v, mem, (add2, j + 1), (ag_done, j))
                        v.bn_stats(stat[:, :], xj).then_inc(bn_done, 1)
                        wait_apart(v, mem, (bn_done, j + 1), (xn_done, j if q == 0 else 0))
                        v.bn_aggr(mv[:, q, :], stat[:, :]).then_inc(ag_done, 1)
                        if q == 3:
                            v.wait_ge(ag_done, j + 1)
                            rsqrt_group(v, nw, 12 * (turn - 1), mv[:, :, 1], nt[:, :], na[:, :], rstd[:, :])
                            v.wait_ge(nw, 12 * turn)
                            for qq in range(4):
                                xq = X[:, bass.ds(j - 3 + qq, 1), :].rearrange("p o d -> p (o d)")
                                wait(v, xt_ready, turn - 1)
                                wait(v, xc_done, 4 * (turn - 1))
                                v.tensor_scalar(xs[qq][:, :], xq, mv[:, qq, 0:1], rstd[:, qq:qq + 1], ALU.subtract, ALU.mult).then_inc(xn_done, 1)

                four_steps(v, 0, 8, NT, NT + 1, body)

            @block.tensor
            def _(pe):
                transpose_group(pe, NT // 4, xs, ident, bT, xn_done, xt_ready, xt_read)

            @block.scalar
            def _(act):
                store_group(act, NT // 4, XT, bT, xt_ready, xt_read)

            @block.gpsimd
            def _(pool):
                def body(n, m, turn):
                    p = m % 2
                    wait_apart(pool, mem, (gix_ready, 2 * (n + 1)), (add2, n - 1))
                    for k in range(2):
                        pool.indirect_dma_start(out=got[p][k][:, :], out_offset=None, in_=mem["outs"],
                                                in_offset=bass.IndirectOffsetOnAxis(ap=gix[p][k][:, 0:1], axis=0)).then_inc(came[p][k], 16)

                    if m == 3:
                        keep_group(pool, turn, X, xs, xn_done, xc_done)

                four_steps(pool, 0, 4, NT, NT, body)
                pool.wait_ge(xc_done, NT)


def transpose_group(pe, groups, xs, ident, bT, xn_done, xt_ready, xt_read):
    def body(q):
        wait(pe, xt_read, 2 * q)
        for k in range(4):
            wait(pe, xn_done, 4 * q + k + 1)
            for g in range(G):
                mm = pe.transpose(bT[g][:, k * P:(k + 1) * P], xs[k][:, g * P:(g + 1) * P], ident[:, :])
        mm.then_inc(xt_ready, 1)

    blocks(pe, groups, body)


def store_group(act, groups, XT, bT, xt_ready, xt_read):
    def body(q):
        wait(act, xt_ready, q + 1)
        for g in range(G):
            act.activation(XT[:, g, bass.ds(q * 512, 512)], bT[g][:, :], ACT.Copy).then_inc(xt_read, 1)

    blocks(act, groups, body)


def keep_group(pool, q, X, xs, xn_done, xc_done):
    for k in range(4):
        pool.wait_ge(xn_done, 4 * q + k + 1)
        pool.tensor_copy(X[:, bass.ds(4 * q + k, 1), :].rearrange("p o d -> p (o d)"), xs[k][:, :]).then_inc(xc_done, 1)


NB = NTOK // 512


def plane(pe, banks, W, rhs, col=0):
    for o in range(G):
        for i in range(G):
            mm = pe.matmul(banks[o][:, :], W[:, i, col + o * P:col + (o + 1) * P], rhs(i), start=(i == 0), stop=(i == G - 1))
    return mm


def build_memory_grad(nc, io, mem):
    XT, ident = mem["XT"], mem["ident"]
    with ExitStack() as c2:
        def sb(name, shape, dt=F32):
            return c2.enter_context(nc.sbuf_tensor("m_" + name, shape, dt))

        def sem(name):
            return c2.enter_context(nc.semaphore("m_" + name))

        def bank(name):
            return c2.enter_context(nc.psum_tensor("m_" + name, [P, 512], F32))

        Wk, Wv, W1, W2, W2T = (sb(k, [P, G, D]) for k in ("Wk", "Wv", "W1", "W2", "W2T"))
        Wlr = sb("Wlr", [P, G])
        lr_w = sb("lr_w", [P, G, P])
        ones = sb("ones", [P, P])
        zb = sb("zb", [P, 512], BF16)
        bias = sb("bias", [P, 4, G])
        blr = sb("blr", [P, 1])
        h0, h1, vb, s1, s2, sl, dv1, dv2, u, dz2, dz1 = (sb(k, [P, G, 512]) for k in ("h0", "h1", "vb", "s1", "s2", "sl", "dv1", "dv2", "u", "dz2", "dz1"))
        alr = sb("alr", [P, 512])
        tok = {k: sb("t_" + k, [P, 4, D]) for k in ("h0", "h1", "dz2", "dz1")}
        bsum = sb("bsum", [P, 4])
        btmp = sb("btmp", [P, 4])
        gw = [sb(f"gw{k}", [P, 512]) for k in range(2)]
        ga = sb("ga", [P, 512])
        PA, PB, PT = [bank("PA0"), bank("PA1")], [bank("PB0"), bank("PB1")], [bank("PT0"), bank("PT1")]
        gW = [bank("gW1"), bank("gW2")]
        w_in, init = sem("w_in"), sem("init")
        k_ready, k_read, v_ready, v_read, lr_ready, lr_read = (sem(k) for k in ("k_ready", "k_read", "v_ready", "v_read", "lr_ready", "lr_read"))
        z1_ready, s1_done, sl1_done, h1_done, w1_done, dv1_done = (sem(k) for k in ("z1_ready", "s1_done", "sl1_done", "h1_done", "w1_done", "dv1_done"))
        z2_ready, s2_done, sl2_done, u_done, t_done, dp_done, w2_done, dv2_done, dz2_done = (
            sem(k) for k in ("z2_ready", "s2_done", "sl2_done", "u_done", "t_done", "dp_done", "w2_done", "dv2_done", "dz2_done"))
        dh_ready, dh_done, dz1_done, bsum_done = sem("dh_ready"), sem("dh_done"), sem("dz1_done"), sem("bsum_done")
        t_ready, t_read, g_ready, upd = sem("t_ready"), sem("t_read"), sem("g_ready"), sem("upd")
        CNST = 0.1 * 2.0 / D

        with nc.Block() as block:
            @block.sync
            def _(sp):
                for dst, name in ((Wk, "m_Wk"), (Wv, "m_Wv"), (W1, "m_W1"), (W2, "m_W2"), (W2T, "m_W2T")):
                    sp.dma_start(dst[:, :, :], io[name].rearrange("(g p) n -> p g n", p=P)).then_inc(w_in, 16)
                sp.dma_start(bias[:, :, :], io["m_bias"]).then_inc(w_in, 16)
                sp.dma_start(Wlr[:, :], io["m_Wlr"]).then_inc(w_in, 16)
                sp.dma_start(blr[:, :], io["m_blr"]).then_inc(w_in, 16)

            @block.tensor
            def _(pe):
                pe.wait_ge(w_in, 16 * 8)
                pe.wait_ge(init, 5)
                for k in range(2):
                    pe.matmul(gW[k][:, :], zb[:, 0:P], zb[:, :], start=True, stop=False, skip_group_check=True)

                def body(q):
                    def x(i):
                        return XT[:, i, bass.ds(q * 512, 512)]

                    def turn_tok(src, done, need, count):
                        wait(pe, done, need)
                        wait(pe, t_read, 2 * (4 * q + count))
                        if count == 0:
                            wait(pe, lr_read, q + 1)
                        for k in range(4):
                            for g in range(G):
                                mm = pe.transpose(PT[k // 2][:, (k % 2) * D + g * P:(k % 2) * D + (g + 1) * P],
                                                  src[:, g, k * P:(k + 1) * P], ident[:, :])
                        mm.then_inc(t_ready, 1)

                    def grad(k, left, right, need):
                        wait(pe, t_read, 2 * (4 * q + need))
                        for t in range(4):
                            for i in range(G):
                                mm = pe.matmul(gW[k][:, i * D:(i + 1) * D], tok[left][:, t, i * P:(i + 1) * P], tok[right][:, t, :],
                                               start=False, stop=False, skip_group_check=True)
                        mm.then_inc(g_ready, 1)

                    wait(pe, dh_done, 2 * q)
                    plane(pe, PA, Wk, x).then_inc(k_ready, 1)
                    wait(pe, sl2_done, 2 * q)
                    plane(pe, PB, Wv, x).then_inc(v_ready, 1)
                    wait(pe, t_read, 8 * q)
                    for g in range(G):
                        mm = pe.matmul(PT[0][:, :], lr_w[:, g, :], x(g), start=(g == 0), stop=(g == G - 1))
                    mm.then_inc(lr_ready, 1)
                    wait(pe, k_read, 2 * (q + 1))
                    plane(pe, PA, W1, lambda i: h0[:, i, :]).then_inc(z1_ready, 1)
                    turn_tok(h0, k_read, 2 * (q + 1), 0)
                    wait(pe, v_read, 2 * (q + 1))
                    wait(pe, h1_done, 2 * (q + 1))
                    plane(pe, PB, W2, lambda i: h1[:, i, :]).then_inc(z2_ready, 1)
                    turn_tok(h1, h1_done, 2 * (q + 1), 1)
                    wait(pe, dz2_done, 2 * (q + 1))
                    wait(pe, sl1_done, 2 * (q + 1))
                    plane(pe, PA, W2T, lambda i: dz2[:, i, :]).then_inc(dh_ready, 1)
                    turn_tok(dz2, dz2_done, 2 * (q + 1), 2)
                    grad(1, "h1", "dz2", 3)
                    turn_tok(dz1, dz1_done, 2 * (q + 1), 3)
                    grad(0, "h0", "dz1", 4)

                blocks(pe, NB, body)

            @block.scalar
            def _(act):
                act.wait_ge(w_in, 16 * 8)
                def body(q):
                    def tok_copy(name, count):
                        wait(act, t_ready, 4 * q + count + 1)
                        wait(act, g_ready, 2 * q)
                        for k in range(2):
                            act.activation(tok[name][:, 2 * k:2 * k + 2, :].rearrange("p t d -> p (t d)"), PT[k][:, :], ACT.Copy).then_inc(t_read, 1)

                    wait(act, k_ready, q + 1)
                    wait(act, h1_done, 2 * q)
                    wait(act, t_ready, 4 * q)
                    for g in range(G):
                        act.activation(h0[:, g, :], PA[g][:, :], ACT.Identity, bias=bias[:, 0, g:g + 1]).then_inc(k_read, 1)
                    wait(act, v_ready, q + 1)
                    wait(act, t_done, 2 * q)
                    for g in range(G):
                        act.activation(vb[:, g, :], PB[g][:, :], ACT.Identity, bias=bias[:, 1, g:g + 1]).then_inc(v_read, 1)
                    wait(act, lr_ready, q + 1)
                    wait(act, dp_done, 2 * q)
                    act.activation(alr[:, :], PT[0][:, :], ACT.Sigmoid, bias=blr[:, 0:1]).then_inc(lr_read, 1)
                    wait(act, z1_ready, q + 1)
                    wait(act, w1_done, 2 * q)
                    wait(act, dv1_done, 2 * q)
                    for g in range(G):
                        act.activation(s1[:, g, :], PA[g][:, :], ACT.Sigmoid, bias=bias[:, 2, g:g + 1]).then_inc(s1_done, 1)
                    tok_copy("h0", 0)
                    wait(act, z2_ready, q + 1)
                    wait(act, w2_done, 2 * q)
                    wait(act, dv2_done, 2 * q)
                    for g in range(G):
                        act.activation(s2[:, g, :], PB[g][:, :], ACT.Sigmoid, bias=bias[:, 3, g:g + 1]).then_inc(s2_done, 1)
                    tok_copy("h1", 1)
                    tok_copy("dz2", 2)
                    tok_copy("dz1", 3)

                blocks(act, NB, body)

            @block.vector
            def _(v):
                v.memset(ones[:, :], 1.0).then_inc(init, 1)
                v.memset(zb[:, :], 0.0).then_inc(init, 1)
                v.memset(bsum[:, :], 0.0).then_inc(init, 1)
                v.wait_ge(w_in, 16 * 8)
                v.wait_ge(init, 3)
                for g in range(G):
                    v.tensor_scalar(lr_w[:, g, :], ones[:, :], Wlr[:, g:g + 1], None, ALU.mult).then_inc(init, 1)

                def body(q):
                    wait(v, s1_done, 2 * (q + 1))
                    for g in range(G):
                        v.scalar_tensor_tensor(out=sl[:, g, :], in0=PA[g][:, :], scalar=bias[:, 2, g:g + 1], in1=s1[:, g, :],
                                               op0=ALU.add, op1=ALU.mult).then_inc(sl1_done, 1)
                    wait(v, k_read, 2 * (q + 1))
                    wait(v, t_ready, 4 * q)
                    for g in range(G):
                        wait(v, sl1_done, 2 * q + g + 1)
                        v.tensor_tensor(h1[:, g, :], h0[:, g, :], sl[:, g, :], ALU.add).then_inc(h1_done, 1)
                    for g in range(G):
                        v.scalar_tensor_tensor(out=dv1[:, g, :], in0=s1[:, g, :], scalar=-1.0, in1=sl[:, g, :],
                                               op0=ALU.add, op1=ALU.mult).then_inc(w1_done, 1)
                    for g in range(G):
                        wait(v, w1_done, 2 * q + g + 1)
                        v.tensor_tensor(dv1[:, g, :], s1[:, g, :], dv1[:, g, :], ALU.subtract).then_inc(dv1_done, 1)
                    wait(v, s2_done, 2 * (q + 1))
                    wait(v, w1_done, 2 * (q + 1))
                    wait(v, h1_done, 2 * (q + 1))
                    for g in range(G):
                        v.scalar_tensor_tensor(out=sl[:, g, :], in0=PB[g][:, :], scalar=bias[:, 3, g:g + 1], in1=s2[:, g, :],
                                               op0=ALU.add, op1=ALU.mult).then_inc(sl2_done, 1)
                    for g in range(G):
                        wait(v, sl2_done, 2 * q + g + 1)
                        v.tensor_tensor(u[:, g, :], h1[:, g, :], sl[:, g, :], ALU.add).then_inc(u_done, 1)
                    wait(v, v_read, 2 * (q + 1))
                    for g in range(G):
                        wait(v, u_done, 2 * q + g + 1)
                        v.tensor_tensor(u[:, g, :], u[:, g, :], vb[:, g, :], ALU.subtract).then_inc(t_done, 1)
                    wait(v, lr_read, q + 1)
                    for g in range(G):
                        wait(v, t_done, 2 * q + g + 1)
                        v.scalar_tensor_tensor(out=u[:, g, :], in0=u[:, g, :], scalar=CNST, in1=alr[:, :], op0=ALU.mult, op1=ALU.mult).then_inc(dp_done, 1)
                    for g in range(G):
                        v.scalar_tensor_tensor(out=dv2[:, g, :], in0=s2[:, g, :], scalar=-1.0, in1=sl[:, g, :],
                                               op0=ALU.add, op1=ALU.mult).then_inc(w2_done, 1)
                    for g in range(G):
                        wait(v, w2_done, 2 * q + g + 1)
                        v.tensor_tensor(dv2[:, g, :], s2[:, g, :], dv2[:, g, :], ALU.subtract).then_inc(dv2_done, 1)
                    wait(v, dh_ready, q)
                    wait(v, t_ready, 4 * q)
                    wait(v, bsum_done, q)
                    for g in range(G):
                        wait(v, dv2_done, 2 * q + g + 1)
                        wait(v, dp_done, 2 * q + g + 1)
                        v.tensor_tensor_reduce(dz2[:, g, :], u[:, g, :], dv2[:, g, :], 1.0, 0.0, ALU.mult, ALU.add,
                                               btmp[:, 2 + g:3 + g]).then_inc(dz2_done, 1)
                    wait(v, dh_ready, q + 1)
                    for g in range(G):
                        v.tensor_tensor(u[:, g, :], PA[g][:, :], u[:, g, :], ALU.add).then_inc(dh_done, 1)
                    for g in range(G):
                        wait(v, dh_done, 2 * q + g + 1)
                        wait(v, dv1_done, 2 * q + g + 1)
                        v.tensor_tensor_reduce(dz1[:, g, :], u[:, g, :], dv1[:, g, :], 1.0, 0.0, ALU.mult, ALU.add,
                                               btmp[:, g:g + 1]).then_inc(dz1_done, 1)
                    wait(v, dz1_done, 2 * (q + 1))
                    wait(v, dz2_done, 2 * (q + 1))
                    v.tensor_tensor(bsum[:, :], bsum[:, :], btmp[:, :], ALU.add).then_inc(bsum_done, 1)

                blocks(v, NB, body)

                n = 0

                def link(ins):
                    nonlocal n
                    n += 1
                    ins.then_inc(upd, 1)
                    v.wait_ge(upd, n)

                v.wait_ge(bsum_done, NB)
                v.wait_ge(g_ready, 2 * NB)
                for k in range(2):
                    link(v.tensor_copy(gw[k][:, :], gW[k][:, :]))
                flat = [mem["W1n"][:, :, :].rearrange("p g d -> p (g d)"), mem["W2n"][:, :, :].rearrange("p g d -> p (g d)"), mem["bn"][:, :, :].rearrange("p k g -> p (k g)")]
                old = [W1[:, :, :].rearrange("p g d -> p (g d)"), W2[:, :, :].rearrange("p g d -> p (g d)"), bias[:, 2:4, :].rearrange("p k g -> p (k g)")]
                for new, was, gr in zip(flat, old, (gw[0][:, :], gw[1][:, :], bsum[:, :])):
                    a = ga[:, 0:gr.shape[1]]
                    link(v.scalar_tensor_tensor(out=a, in0=gr, scalar=-1.0, in1=gr, op0=ALU.mult, op1=ALU.max))
                    link(v.tensor_scalar(a, a, 1e-8, None, ALU.add))
                    link(v.reciprocal(a, a))
                    link(v.tensor_tensor(a, a, gr, ALU.mult))
                    link(v.tensor_scalar(a, a, -0.01, None, ALU.mult))
                    link(v.scalar_tensor_tensor(out=new, in0=was, scalar=1.0 - 0.01 * 0.01, in1=a, op0=ALU.mult, op1=ALU.add))


def layer_norm_group(v, mem, X, q, src, srcsem, sems, bufs, xs, before_xs):
    bn_done, ag_done, nw, xn_done = sems
    stat, mv, nt, na, rstd = bufs
    for k in range(4):
        xk = X[:, bass.ds(4 * q + k, 1), :].rearrange("p o d -> p (o d)")
        wait_apart(v, mem, (srcsem, src(k)), (ag_done, 4 * q + k))
        v.bn_stats(stat[:, k, :], xk).then_inc(bn_done, 1)
        wait_apart(v, mem, (bn_done, 4 * q + k + 1), (xn_done, 4 * q))
        v.bn_aggr(mv[:, k, :], stat[:, k, :]).then_inc(ag_done, 1)
    wait(v, ag_done, 4 * q + 4)
    rsqrt_group(v, nw, 12 * q, mv[:, :, 1], nt[:, :], na[:, :], rstd[:, :])
    wait(v, nw, 12 * q + 12)
    before_xs()
    for k in range(4):
        xk = X[:, bass.ds(4 * q + k, 1), :].rearrange("p o d -> p (o d)")
        v.tensor_scalar(xs[k][:, :], xk, mv[:, k, 0:1], rstd[:, k:k + 1], ALU.subtract, ALU.mult).then_inc(xn_done, 1)


def build_memory_read(nc, io, mem):
    X, XT, ident, W1n, W2n, bn = mem["X"], mem["XT"], mem["ident"], mem["W1n"], mem["W2n"], mem["bn"]
    with ExitStack() as c2:
        def sb(name, shape, dt=F32):
            return c2.enter_context(nc.sbuf_tensor("q_" + name, shape, dt))

        def sem(name):
            return c2.enter_context(nc.semaphore("q_" + name))

        def bank(name):
            return c2.enter_context(nc.psum_tensor("q_" + name, [P, 512], F32))

        Wq, bq = sb("Wq", [P, G, D]), sb("bq", [P, G])
        h0, h1, h2, s1, s2, sl, sm = (sb(k, [P, G, 512]) for k in ("h0", "h1", "h2", "s1", "s2", "sl", "sm"))
        xs = [sb(f"xs{k}", [P, D]) for k in range(4)]
        bufs = (sb("stat", [P, 4, 6]), sb("mv", [P, 4, 2]), sb("nt", [P, 4]), sb("na", [P, 4]), sb("rstd", [P, 4]))
        PA, PB, PT, PX = ([bank(f"{k}0"), bank(f"{k}1")] for k in ("PA", "PB", "PT", "PX"))
        w_in, q_ready, q_read, z1_ready, s1_done, sl1_done, h1_done = (sem(k) for k in ("w_in", "q_ready", "q_read", "z1_ready", "s1_done", "sl1_done", "h1_done"))
        z2_ready, s2_done, sl2_done, h2_done, t_ready, res_done = (sem(k) for k in ("z2_ready", "s2_done", "sl2_done", "h2_done", "t_ready", "res_done"))
        lns = [sem(k) for k in ("bn_done", "ag_done", "nw", "xn_done")]
        xn_done = lns[3]
        xc_done, xt_ready, xt_read = sem("xc_done"), sem("xt_ready"), sem("xt_read")

        with nc.Block() as block:
            @block.sync
            def _(sp):
                sp.dma_start(Wq[:, :, :], io["m_Wq"].rearrange("(g p) n -> p g n", p=P)).then_inc(w_in, 16)
                sp.dma_start(bq[:, :], io["m_bq"]).then_inc(w_in, 16)

            @block.tensor
            def _(pe):
                pe.wait_ge(w_in, 32)

                def front(q):
                    wait(pe, sl2_done, 2 * q)
                    plane(pe, PA, Wq, lambda i: XT[:, i, bass.ds(q * 512, 512)]).then_inc(q_ready, 1)

                def turn_x(q):
                    wait(pe, xt_read, 2 * q)
                    for k in range(4):
                        pe.wait_ge(xn_done, 4 * q + k + 1)
                        for g in range(G):
                            mm = pe.transpose(PX[g][:, k * P:(k + 1) * P], xs[k][:, g * P:(g + 1) * P], ident[:, :])
                    mm.then_inc(xt_ready, 1)

                def rest(q, last_x):
                    pe.wait_ge(q_read, 2 * (q + 1))
                    wait(pe, sl1_done, 2 * q)
                    plane(pe, PB, W1n, lambda i: h0[:, i, :]).then_inc(z1_ready, 1)
                    if last_x:
                        turn_x(q - 1)
                    pe.wait_ge(h1_done, 2 * (q + 1))
                    plane(pe, PA, W2n, lambda i: h1[:, i, :]).then_inc(z2_ready, 1)
                    pe.wait_ge(h2_done, 2 * (q + 1))
                    wait(pe, res_done, 2 * q)
                    for k in range(4):
                        for g in range(G):
                            mm = pe.transpose(PT[k // 2][:, (k % 2) * D + g * P:(k % 2) * D + (g + 1) * P], h2[:, g, k * P:(k + 1) * P], ident[:, :])
                    mm.then_inc(t_ready, 1)

                front(0)
                rest(0, False)
                with pe.Fori(1, NB) as q:
                    front(q)
                    rest(q, True)
                turn_x(NB - 1)

            @block.scalar
            def _(act):
                act.wait_ge(w_in, 32)

                def body(q, last_x):
                    act.wait_ge(q_ready, q + 1)
                    wait(act, h1_done, 2 * q)
                    for g in range(G):
                        act.activation(h0[:, g, :], PA[g][:, :], ACT.Identity, bias=bq[:, g:g + 1]).then_inc(q_read, 1)
                    act.wait_ge(z1_ready, q + 1)
                    for g in range(G):
                        act.activation(s1[:, g, :], PB[g][:, :], ACT.Sigmoid, bias=bn[:, 0, g:g + 1]).then_inc(s1_done, 1)
                    act.wait_ge(z2_ready, q + 1)
                    for g in range(G):
                        act.activation(s2[:, g, :], PA[g][:, :], ACT.Sigmoid, bias=bn[:, 1, g:g + 1]).then_inc(s2_done, 1)
                    if last_x:
                        store(q - 1)

                def store(q):
                    act.wait_ge(xt_ready, q + 1)
                    for g in range(G):
                        act.activation(XT[:, g, bass.ds(q * 512, 512)], PX[g][:, :], ACT.Copy).then_inc(xt_read, 1)

                body(0, False)
                with act.Fori(1, NB) as q:
                    body(q, True)
                store(NB - 1)

            @block.vector
            def _(v):
                def body(q):
                    wait(v, s1_done, 2 * (q + 1))
                    for g in range(G):
                        v.scalar_tensor_tensor(out=sl[:, g, :], in0=PB[g][:, :], scalar=bn[:, 0, g:g + 1], in1=s1[:, g, :],
                                               op0=ALU.add, op1=ALU.mult).then_inc(sl1_done, 1)
                    for g in range(G):
                        wait(v, sl1_done, 2 * q + g + 1)
                        v.tensor_tensor(h1[:, g, :], h0[:, g, :], sl[:, g, :], ALU.add).then_inc(h1_done, 1)
                    wait(v, s2_done, 2 * (q + 1))
                    for g in range(G):
                        v.scalar_tensor_tensor(out=sm[:, g, :], in0=PA[g][:, :], scalar=bn[:, 1, g:g + 1], in1=s2[:, g, :],
                                               op0=ALU.add, op1=ALU.mult).then_inc(sl2_done, 1)
                    wait(v, t_ready, q)
                    for g in range(G):
                        wait(v, sl2_done, 2 * q + g + 1)
                        v.tensor_tensor(h2[:, g, :], h1[:, g, :], sm[:, g, :], ALU.add).then_inc(h2_done, 1)
                    wait(v, t_ready, q + 1)
                    for k in range(2):
                        xk = X[:, bass.ds(4 * q + 2 * k, 2), :].rearrange("p o d -> p (o d)")
                        v.tensor_tensor(xk, PT[k][:, :], xk, ALU.add).then_inc(res_done, 1)

                    def free():
                        wait(v, xt_ready, q)
                        wait(v, xc_done, 4 * q)

                    layer_norm_group(v, mem, X, q, lambda k: 2 * q + k // 2 + 1, res_done, lns, bufs, xs, free)

                blocks(v, NB, body)

            @block.gpsimd
            def _(pool):
                def body(q):
                    keep_group(pool, q, X, xs, xn_done, xc_done)

                blocks(pool, NB, body)
                pool.wait_ge(xc_done, NT)


def build_ternary_mlp(nc, io, mem, out):
    X, XT = mem["X"], mem["XT"]
    FC = 4 * D // P
    with ExitStack() as c2:
        def sb(name, shape, dt=F32):
            return c2.enter_context(nc.sbuf_tensor("t_" + name, shape, dt))

        def sem(name):
            return c2.enter_context(nc.semaphore("t_" + name))

        def bank(name):
            return c2.enter_context(nc.psum_tensor("t_" + name, [P, 512], F32))

        W1, W2 = sb("W1", [P, G, 4 * D]), sb("W2", [P, FC, D])
        b1, b2 = sb("b1", [P, FC]), sb("b2", [P, D])
        ones = sb("ones", [P, P])
        sums = sb("sums", [P, 2])
        gam = sb("gam", [P, 2])
        hT = [sb(f"hT{p}", [P, FC, 512]) for p in range(2)]
        xo = [sb(f"xo{k}", [P, D]) for k in range(4)]
        bufs = (sb("stat", [P, 4, 6]), sb("mv", [P, 4, 2]), sb("nt", [P, 4]), sb("na", [P, 4]), sb("rstd", [P, 4]))
        bH, bO, bS = [bank(f"bH{k}") for k in range(4)], [bank("bO0"), bank("bO1")], bank("bS")
        flat = [W1[:, :, :].rearrange("p g n -> p (g n)"), W2[:, :, :].rearrange("p g n -> p (g n)")]
        PREP = 11
        w_in, prep, s_ready, h_ready, h_read, o_ready, o_read, b_done = (sem(k) for k in ("w_in", "prep", "s_ready", "h_ready", "h_read", "o_ready", "o_read", "b_done"))
        lns = [sem(k) for k in ("bn_done", "ag_done", "nw", "xn_done")]
        xn_done, y_out = lns[3], [sem(f"y_out{k}") for k in range(4)]

        with nc.Block() as block:
            @block.sync
            def _(sp):
                sp.dma_start(W1[:, :, :], io["t_W1T"].rearrange("(g p) n -> p g n", p=P)).then_inc(w_in, 16)
                sp.dma_start(W2[:, :, :], io["t_W2T"].rearrange("(g p) n -> p g n", p=P)).then_inc(w_in, 16)
                sp.dma_start(b1[:, :], io["t_b1"]).then_inc(w_in, 16)
                sp.dma_start(b2[:, :], io["t_b2"].rearrange("(o n) -> o n", o=1).to_broadcast([P, D])).then_inc(w_in, 16)
                def body(q):
                    for k in range(4):
                        wait(sp, xn_done, 4 * q + k + 1)
                        sp.dma_start(out[k, bass.ds(q * P, P), :], xo[k][:, :]).then_inc(y_out[k], 16)

                blocks(sp, NB, body)
                for k in range(4):
                    sp.wait_ge(y_out[k], 16 * NB)

            @block.tensor
            def _(pe):
                pe.wait_ge(prep, 3)
                pe.matmul(bS[:, 0:2], ones[:, :], sums[:, :], start=True, stop=True).then_inc(s_ready, 1)
                pe.wait_ge(prep, PREP)
                pe.wait_ge(w_in, 64)

                def up(q, p):
                    for f in range(FC):
                        wait(pe, h_read, FC * q + f - 3)
                        for g in range(G):
                            mm = pe.matmul(bH[f % 4][:, :], W1[:, g, f * P:(f + 1) * P], XT[:, g, bass.ds(q * 512, 512)],
                                           start=(g == 0), stop=(g == G - 1))
                        mm.then_inc(h_ready, 1)

                def down(q, p):
                    pe.wait_ge(h_read, FC * (q + 1))
                    for k in range(4):
                        wait(pe, o_read, 4 * q + k - 1)
                        for f in range(FC):
                            mm = pe.matmul(bO[k % 2][:, 0:D], hT[p][:, f, k * P:(k + 1) * P], W2[:, f, :], start=(f == 0), stop=(f == FC - 1))
                        mm.then_inc(o_ready, 1)

                up(0, 0)
                up(1, 1)
                down(0, 0)
                with pe.Fori(1, NB // 2) as j:
                    up(2 * j, 0)
                    down(2 * j - 1, 1)
                    up(2 * j + 1, 1)
                    down(2 * j, 0)
                down(NB - 1, 1)

            @block.scalar
            def _(act):
                act.wait_ge(w_in, 64)

                def body(q, p):
                    wait(act, o_ready, 4 * (q - 1))
                    for f in range(FC):
                        act.wait_ge(h_ready, FC * q + f + 1)
                        act.activation(hT[p][:, f, :], bH[f % 4][:, :], ACT.Relu, bias=b1[:, f:f + 1]).then_inc(h_read, 1)

                body(0, 0)
                body(1, 1)
                with act.Fori(1, NB // 2) as j:
                    body(2 * j, 0)
                    body(2 * j + 1, 1)

            @block.vector
            def _(v):
                n = 0

                def link(ins):
                    nonlocal n
                    n += 1
                    ins.then_inc(prep, 1)
                    v.wait_ge(prep, n)

                v.wait_ge(w_in, 64)
                link(v.memset(ones[:, :], 1.0))
                for k in range(2):
                    link(v.tensor_reduce(sums[:, k:k + 1], flat[k], AX.X, ALU.add, apply_absolute_value=True))
                v.wait_ge(s_ready, 1)
                link(v.tensor_scalar(gam[:, :], bS[:, 0:2], 1.0 / (4 * D * D), 1e-5, ALU.mult, ALU.add))
                link(v.reciprocal(gam[:, :], gam[:, :]))
                for a, opa, b, opb in ((None, ALU.mult, 1.0, ALU.min), (-1.0, ALU.max, 12582912.0, ALU.add), (-12582912.0, ALU.add, 0.0, ALU.add)):
                    for k in range(2):
                        link(v.tensor_scalar(flat[k], flat[k], gam[:, k:k + 1] if a is None else a, b, opa, opb))
                assert n == PREP

                def body(q):
                    for k in range(4):
                        xk = X[:, bass.ds(4 * q + k, 1), :].rearrange("p o d -> p (o d)")
                        v.tensor_tensor(xk, b2[:, :], xk, ALU.add).then_inc(b_done, 1)
                    for k in range(4):
                        xk = X[:, bass.ds(4 * q + k, 1), :].rearrange("p o d -> p (o d)")
                        wait(v, o_ready, 4 * q + k + 1)
                        wait(v, b_done, 4 * q + k + 1)
                        v.tensor_tensor(xk, bO[k % 2][:, 0:D], xk, ALU.add).then_inc(o_read, 1)

                    def free():
                        for k in range(4):
                            wait(v, y_out[k], 16 * q)

                    layer_norm_group(v, mem, X, q, lambda k: 4 * q + k + 1, o_read, lns, bufs, xo, free)

                blocks(v, NB, body)


def rsqrt_group(v, sem, base, var, t, a, y):
    step = 0

    def link(ins):
        nonlocal step
        step += 1
        ins.then_inc(sem, 1)
        if step < 12:
            v.wait_ge(sem, base + step)

    link(v.tensor_scalar(t, var, EPS, None, ALU.add))
    link(v.tensor_scalar(a.bitcast(I32), t.bitcast(I32), 1, None, ALU.arith_shift_right))
    link(v.tensor_scalar(y.bitcast(I32), a.bitcast(I32), -1.0, float(0x5F3759DF), ALU.mult, ALU.add))
    for _ in range(3):
        link(v.tensor_tensor(a, y, y, ALU.mult))
        link(v.scalar_tensor_tensor(out=a, in0=a, scalar=-0.5, in1=t, op0=ALU.mult, op1=ALU.mult))
        link(v.scalar_tensor_tensor(out=y, in0=a, scalar=1.5, in1=y, op0=ALU.add, op1=ALU.mult))


def clear_released(nc):
    ids = sorted(nc.released_uncleared_semaphores)
    with nc.Block() as block:
        @block.gpsimd
        def _(pool):
            start = 0
            for k in range(1, len(ids) + 1):
                if k == len(ids) or ids[k] != ids[k - 1] + 1:
                    pool.sem_clear(range(ids[start], ids[k - 1] + 1))
                    start = k


def build(nc, io, out):
    with ExitStack() as ctx:
        def sb(name, shape, dt=F32):
            return ctx.enter_context(nc.sbuf_tensor(name, shape, dt))

        mem = {
            "X": sb("X", [P, NT, D]),
            "ident": sb("ident", [P, P]),
            "Etok": sb("Etok", [P, NC, P]),
            "dec": sb("dec", [P, G, B * NC]),
            "score": sb("score", [P, NT, E8]),
            "topv": sb("topv", [P, NT, E8]),
            "topi": sb("topi", [P, NT, E8], U32),
            "slot": sb("slot", [P, 2, NT], U32),
            "expert": sb("expert", [1, NI], I32),
            "rows": nc.dram_tensor("rows", (NI * P, D), F32, kind="Internal").ap(),
            "outs": nc.dram_tensor("outs", (NI * P, D), F32, kind="Internal").ap(),
            "g_parts": nc.dram_tensor("g_parts", (3, P, S), BF16, kind="Internal").ap(),
        }
        mem["begun"] = ctx.enter_context(nc.semaphore("begun"))
        build_gates(nc, ctx, io, mem)
        experts = ctx.enter_context(ExitStack())
        mem["Win"] = experts.enter_context(nc.sbuf_tensor("Win", [P, E8 + 1, G, F], F32))
        mem["Wsw"] = experts.enter_context(nc.sbuf_tensor("Wsw", [P, E8 + 1, G, F], F32))
        build_attention(nc, ctx, io, mem)
        mem["Wout"] = experts.enter_context(nc.sbuf_tensor("Wout", [P, E8 + 1, 4, D], F32))
        build_shared_and_routes(nc, io, mem)
        build_expert_tiles(nc, mem, "ro_", NI, shared=False)
        experts.close()
        clear_released(nc)
        mem["XT"] = sb("XT", [P, G, NTOK])
        build_combine(nc, mem)
        mem["W1n"], mem["W2n"], mem["bn"] = sb("W1n", [P, G, D]), sb("W2n", [P, G, D]), sb("bn", [P, 2, G])
        build_memory_grad(nc, io, mem)
        build_memory_read(nc, io, mem)
        build_ternary_mlp(nc, io, mem, out)


def kernel(**inputs):
    import numpy as np
    import concourse.bacc as bacc
    from concourse import mybir as mb
    from concourse.bass_utils import run_bass_kernel_spmd as run

    a = {k: np.asarray(v) for k, v in inputs.items()}
    order = np.array([8 * g + 2 * r + e for r in range(4) for g in range(2) for e in range(2)])
    rows = (order[:, None] * DH + np.arange(DH)).reshape(-1)
    p = np.arange(P)
    hh = np.array([[(q // 32) * 4 + g * 2 + (q % 32) // 16 for q in range(P)] for g in range(G)])

    def columns(v):
        return v.reshape(-1, P).T

    arrays = {
        "x": a["L0_attn_x"],
        "xT": a["L0_attn_x"].reshape(NTOK, D).T,
        "WqT": a["L0_attn_Wq"].T, "WkT": a["L0_attn_Wk"].T,
        "WvT": a["L0_attn_Wv"][rows].T, "WoT": a["L0_attn_Wo"][:, rows].T,
        "WgT": a["L0_attn_Wg"][order].T, "bg": a["L0_attn_bg"][order],
        "router": a["L0_ffn_router_DE"],
        "w_in": np.concatenate([a["L0_ffn_w_in_eDF"], a["L0_ffn_w_in_shared_FD"].T[None]]),
        "w_sw": np.concatenate([a["L0_ffn_w_swiglu_eDF"], a["L0_ffn_w_swiglu_FD"].T[None]]),
        "w_out": np.concatenate([a["L0_ffn_w_out_eFD"], a["L0_ffn_w_out_shared_DF"].T[None]]),
        "m_Wk": a["L1_attn_Wk"], "m_Wv": a["L1_attn_Wv"], "m_Wq": a["L1_attn_Wq"], "m_W1": a["L1_attn_W1"], "m_W2": a["L1_attn_W2"],
        "m_W2T": a["L1_attn_W2"].T, "m_Wlr": columns(a["L1_attn_Wlr"][:, 0]), "m_blr": np.tile(a["L1_attn_blr"], (P, 1)), "m_bq": columns(a["L1_attn_bq"]),
        "m_bias": np.stack([columns(a[f"L1_attn_{k}"]) for k in ("bk", "bv", "b1", "b2")], axis=1),
        "t_W1T": a["L1_ffn_W1"].T, "t_W2T": a["L1_ffn_W2"].T, "t_b1": columns(a["L1_ffn_b1"]), "t_b2": a["L1_ffn_b2"],
        "iota8": np.tile(np.arange(E8, dtype=np.float32), (P, 1)),
        "item": np.tile(np.arange(NI, dtype=np.float32), (P, 1)),
        "tri": (p[:, None] < p[None, :]).astype(np.float32),
        "ident": np.eye(P, dtype=np.float32),
        "rep": np.stack([(p[:, None] % 32 == hh[g][None, :]) for g in range(G)]).astype(np.float32),
        "bmask": (p[:, None] // 32 == np.arange(B)[None, :]).astype(np.float32),
        "hmask": ((p[:, None] // 16) % 2 == np.arange(2)[None, :]).astype(np.float32),
        "blk": np.stack([(p[:, None] // 16 == p[None, :] // 16)] * G).astype(np.float32),
    }
    nc = bacc.Bacc("TRN2", target_bir_lowering=False, num_devices=1)
    io, feed = {}, {}
    for k, v in arrays.items():
        v = np.ascontiguousarray(v)
        feed[f"in_{k}"] = v
        io[k] = nc.dram_tensor(f"in_{k}", v.shape, mb.dt.from_np(v.dtype), kind="ExternalInput").ap()
    out = nc.dram_tensor("out", (B, S, D), F32, kind="ExternalOutput").ap()
    build(nc, io, out)
    r = run(nc, [feed], core_ids=[0])
    return r.results[0]["out"]
```

```python
from contextlib import ExitStack

import concourse.bass as bass
from concourse import mybir

F32 = mybir.dt.float32
F32R = mybir.dt.float32r
BF16 = mybir.dt.bfloat16
I32 = mybir.dt.int32
U32 = mybir.dt.uint32
ALU = mybir.AluOpType
ACT = mybir.ActivationFunctionType
AX = mybir.AxisListType

P = 128
B, S, D = 4, 1024, 256
NTOK = B * S
NT = NTOK // P
NC = S // P
G = D // P
H, DH = 16, 16
E8 = 8
F = 512
EPS = 1e-5
NI = 72
assert NI >= 2 * NTOK // P + E8 - 1 and NI % 4 == 0


def wait(e, sem, value):
    if isinstance(value, int) and value <= 0:
        return
    e.wait_ge(sem, value)


def wait_apart(e, mem, *waits):
    waits = [(sem, value if isinstance(value, int) else e.to_reg(value)) for sem, value in waits]
    e.wait_ge(mem["begun"], 1)
    for sem, value in waits:
        wait(e, sem, value)


def four_steps(e, lo, main_lo, main_hi, hi, body):
    for n in range(lo, main_lo):
        body(n, n % 4, n // 4)
    with e.Fori(main_lo // 4, main_hi // 4) as turn:
        for m in range(4):
            body(turn * 4 + m, m, turn)
    for n in range(main_hi, hi):
        body(n, n % 4, n // 4)


def blocks(e, count, body):
    body(0)
    with e.Fori(1, count) as q:
        body(q)


def has(n, back, count=NT):
    return not isinstance(n, int) or 0 <= n - back < count


def build_gates(nc, ctx, io, mem):
    def sem(name):
        return ctx2.enter_context(nc.semaphore(name))

    with ExitStack() as ctx2:
        def sb(name, shape, dt=F32):
            return ctx2.enter_context(nc.sbuf_tensor(name, shape, dt))

        gT = sb("g_gT", [P, S])
        d0 = sb("g_d0", [P, S])
        d1 = sb("g_d1", [P, S])
        ET = sb("g_ET", [P, S])
        part = sb("g_part", [P, 3, S], BF16)
        rest1 = sb("g_rest1", [P, S])
        rest2 = sb("g_rest2", [P, S])
        last = sb("g_last", [P, B, NC])
        WgT = sb("g_WgT", [P, G, 32])
        bg = sb("g_bg", [P, 1])
        rep = sb("g_rep", [P, G, P])
        bmask = sb("g_bmask", [P, B])
        xT = sb("g_xT", [P, G, NTOK])
        Z = ctx2.enter_context(nc.psum_tensor("g_Z", [P, 2, 512], F32))
        TP = ctx2.enter_context(nc.psum_tensor("g_TP", [P, NC, P], F32))
        DP = ctx2.enter_context(nc.psum_tensor("g_DP", [P, 512], F32))
        zeroed, wg_in, x_in, cst_in = sem("g_zeroed"), sem("g_wg_in"), [sem(f"g_x_in{b}") for b in range(B)], sem("g_cst_in")
        z_ready, g_ready, dve_step, et_ready = sem("g_z_ready"), sem("g_g_ready"), sem("g_dve_step"), sem("g_et_ready")
        parts_ready, parts_out, tp_ready, last_ready = sem("g_parts_ready"), sem("g_parts_out"), sem("g_tp_ready"), sem("g_last_ready")
        dec_ready, tp_read = sem("g_dec_ready"), sem("g_tp_read")

        with nc.Block() as block:
            @block.sync
            def _(sp):
                sp.wait_ge(zeroed, 2)
                sp.dma_start(WgT[:, :, 0:H], io["WgT"].rearrange("(g p) h -> p g h", p=P)).then_inc(wg_in, 16)
                for b in range(B):
                    sp.dma_start(bg[32 * b:32 * b + H, :], io["bg"].rearrange("(h o) -> h o", o=1)).then_inc(wg_in, 16)
                for b in range(B):
                    sp.dma_start(xT[:, :, b * S:(b + 1) * S],
                                 io["xT"].rearrange("(g p) t -> p g t", p=P)[:, :, b * S:(b + 1) * S]).then_inc(x_in[b], 16)
                sp.dma_start(mem["ident"][:, :], io["ident"]).then_inc(cst_in, 16)
                sp.dma_start(rep[:, :, :], io["rep"].rearrange("g p m -> p g m")).then_inc(cst_in, 16)
                sp.dma_start(bmask[:, :], io["bmask"]).then_inc(cst_in, 16)
                sp.wait_ge(parts_ready, 3)
                sp.dma_start(mem["g_parts"].rearrange("k p s -> p k s"), part[:, :, :]).then_inc(parts_out, 16)
                sp.wait_ge(parts_out, 16)
                sp.wait_ge(cst_in, 48)

            @block.tensor
            def _(pe):
                pe.wait_ge(wg_in, 16 * 5)
                for b in range(B):
                    pe.wait_ge(x_in[b], 16)
                    for half in range(2):
                        for g in range(G):
                            mm = pe.matmul(Z[32 * b:32 * b + 32, half, :], WgT[:, g, :],
                                           xT[:, g, b * S + half * 512:b * S + (half + 1) * 512],
                                           start=(g == 0), stop=(g == G - 1))
                mm.then_inc(z_ready, 1)
                pe.wait_ge(cst_in, 48)
                pe.wait_ge(et_ready, 1)
                for c in range(NC):
                    mm = pe.transpose(TP[:, c, :], ET[:, c * P:(c + 1) * P], mem["ident"][:, :])
                mm.then_inc(tp_ready, 1)
                pe.wait_ge(last_ready, B)
                for g in range(G):
                    mm = pe.matmul(DP[:, g * 32:(g + 1) * 32], rep[:, g, :], last[:, :, :].rearrange("p b c -> p (b c)"),
                                   start=True, stop=True)
                mm.then_inc(dec_ready, 1)

            @block.scalar
            def _(act):
                act.wait_ge(z_ready, 1)
                act.wait_ge(wg_in, 16 * 5)
                act.activation(gT[:, :], Z[:, :, :].rearrange("p a n -> p (a n)"), ACT.Sigmoid, bias=bg[:, 0:1]).then_inc(g_ready, 1)
                act.wait_ge(tp_ready, 1)
                act.activation(mem["Etok"][:, :, :], TP[:, :, :], ACT.Copy).then_inc(tp_read, 1)
                act.wait_ge(tp_read, 1)

            @block.vector
            def _(v):
                v.memset(bg[:, :], 0.0).then_inc(mem["begun"], 1)
                v.wait_ge(mem["begun"], 1)
                v.memset(WgT[:, :, :], 0.0).then_inc(zeroed, 1)
                v.memset(bg[:, :], 0.0).then_inc(zeroed, 1)
                v.memset(d1[:, :], 0.0).then_inc(dve_step, 1)
                v.wait_ge(g_ready, 1)
                v.wait_ge(dve_step, 1)
                v.tensor_copy(d0[:, :], gT[:, :]).then_inc(dve_step, 1)
                v.tensor_copy(d1[:, 0:S:P], gT[:, 0:S:P]).then_inc(dve_step, 1)
                v.tensor_copy(part[:, 0, :], gT[:, :]).then_inc(parts_ready, 1)
                v.wait_ge(dve_step, 3)
                v.memset(d0[:, 0:S:P], 0.0).then_inc(dve_step, 1)
                v.wait_ge(dve_step, 4)
                v.tensor_tensor_scan(ET[:, :], d0[:, :], d1[:, :], 0.0, ALU.mult, ALU.add).then_inc(et_ready, 1)
                v.wait_ge(parts_ready, 1)
                v.tensor_tensor(rest1[:, :], gT[:, :], part[:, 0, :], ALU.subtract).then_inc(dve_step, 1)
                v.wait_ge(dve_step, 5)
                v.tensor_copy(part[:, 1, :], rest1[:, :]).then_inc(parts_ready, 1)
                v.wait_ge(parts_ready, 2)
                v.tensor_tensor(rest2[:, :], rest1[:, :], part[:, 1, :], ALU.subtract).then_inc(dve_step, 1)
                v.wait_ge(dve_step, 6)
                v.tensor_copy(part[:, 2, :], rest2[:, :]).then_inc(parts_ready, 1)
                v.wait_ge(et_ready, 1)
                v.wait_ge(cst_in, 48)
                for b in range(B):
                    v.tensor_scalar(last[:, b, :], ET[:, P - 1:S:P], bmask[:, b:b + 1], None, ALU.mult).then_inc(last_ready, 1)
                v.wait_ge(dec_ready, 1)
                v.tensor_copy(mem["dec"][:, :, :], DP[:, 0:G * 32].rearrange("p (g n) -> p g n", g=G)).then_inc(dve_step, 1)
                v.wait_ge(dve_step, 7)


def build_attention(nc, ctx, io, mem):
    X, ident = mem["X"], mem["ident"]
    with ExitStack() as c2:
        def sb(name, shape, dt=F32):
            return c2.enter_context(nc.sbuf_tensor("a_" + name, shape, dt))

        def sem(name):
            return c2.enter_context(nc.semaphore("a_" + name))

        def bank(name):
            return c2.enter_context(nc.psum_tensor("a_" + name, [P, 512], F32))

        Wqk = sb("Wqk", [P, G, 2 * D])
        Wv = sb("Wv", [P, G, D])
        Wo = sb("Wo", [P, G, D])
        Wr = sb("Wr", [P, G, E8])
        hmask = sb("hmask", [P, 2])
        blk = sb("blk", [P, G, P])
        ones3 = sb("ones3", [3, P], BF16)
        xt = [sb(f"xt{p}", [P, G, P]) for p in range(2)]
        gr = [sb(f"gr{p}", [3, H * P], BF16) for p in range(2)]
        eqk = sb("eqk", [P, 2 * D])
        rqk = sb("rqk", [P, 2 * D])
        qk = [sb(f"qk{p}", [P, 2, G, P]) for p in range(2)]
        kh = [sb(f"kh{p}", [P, 2, G, P]) for p in range(2)]
        vt = [sb(f"vt{p}", [P, D]) for p in range(2)]
        dcy = [sb(f"dcy{p}", [P, H, P]) for p in range(2)]
        A = sb("A", [P, H, P])
        kw = sb("kw", [P, D])
        ye = sb("ye", [P, D])
        y = sb("y", [P, D])
        yT = sb("yT", [P, G, P])
        um = sb("um", [P, G, P])
        St = sb("St", [P, B, G, P])
        Sd = sb("Sd", [P, G, P])
        stat = sb("stat", [P, 6])
        mv = sb("mv", [P, 4, 2])
        nt = sb("nt", [P, 4])
        na = sb("na", [P, 4])
        rstd = sb("rstd", [P, 4])
        xn = [sb(f"xn{p}", [P, D]) for p in range(2)]
        xnT = sb("xnT", [P, G, P])
        bQK, bS, bZ = bank("bQK"), [bank("bS0"), bank("bS1")], [bank("bZ0"), bank("bZ1")]
        bM0, bM1, bM2 = bank("bM0"), bank("bM1"), bank("bM2")

        zero = sb("zero", [P, D])
        w_in, init, ex_in = sem("w_in"), sem("init"), sem("ex_in")
        xt_in = [sem("xt_in0"), sem("xt_in1")]
        gr_in = [sem("gr_in0"), sem("gr_in1")]
        qk_ready, qk_read, act_phi, phi_done, km_done = sem("qk_ready"), sem("qk_read"), sem("act_phi"), sem("phi_done"), sem("km_done")
        v_ready, v_read, z_ready, d_done, s_ready, a_done, av_done = (sem(k) for k in ("v_ready", "v_read", "z_ready", "d_done", "s_ready", "a_done", "av_done"))
        kt_ready, kw_done, y2_done, ye_done, y_done = (sem(k) for k in ("kt_ready", "kw_done", "y2_done", "ye_done", "y_done"))
        yt_ready, yt_read, o_ready, res_done, bn_done, ag_done = (sem(k) for k in ("yt_ready", "yt_read", "o_ready", "res_done", "bn_done", "ag_done"))
        u_ready, um_done, sd_done, st_step, nw = (sem(k) for k in ("u_ready", "um_done", "sd_done", "st_step", "newton"))
        xn_done, xnt_ready, xnt_read, xc_done, r_ready, r_read, mx_done, mi_done = (
            sem(k) for k in ("xn_done", "xnt_ready", "xnt_read", "xc_done", "r_ready", "r_read", "mx_done", "mi_done"))
        NWT = 12

        LO, ML, MH, HI = 0, 8, NT, NT + 7
        QK_READS = 2

        with nc.Block() as block:
            @block.sync
            def _(sp):
                for dst, name in ((Wv, "WvT"), (Wo, "WoT"), (Wr, "router")):
                    sp.dma_start(dst[:, :, :], io[name].rearrange("(g p) n -> p g n", p=P)).then_inc(w_in, 16)
                sp.dma_start(Wqk[:, :, 0:D], io["WqT"].rearrange("(g p) n -> p g n", p=P)).then_inc(w_in, 16)
                sp.dma_start(Wqk[:, :, D:2 * D], io["WkT"].rearrange("(g p) n -> p g n", p=P)).then_inc(w_in, 16)
                sp.dma_start(hmask[:, :], io["hmask"]).then_inc(w_in, 16)
                sp.dma_start(blk[:, :, :], io["blk"].rearrange("g p n -> p g n")).then_inc(w_in, 16)
                sp.dma_start(X[:, :, :].rearrange("p (c b) d -> p c b d", b=B)[:, :, 0, :],
                             io["x"][0].rearrange("(c p) d -> p c d", p=P)).then_inc(w_in, 16)
                for b in range(1, B):
                    sp.dma_start(X[:, :, :].rearrange("p (c b) d -> p c b d", b=B)[:, :, b, :],
                                 io["x"][b].rearrange("(c p) d -> p c d", p=P)).then_inc(w_in, 16)

                def body(n, m, turn):
                    if not has(n, 0):
                        return
                    p = m % 2
                    wait(sp, v_ready, n - 1)
                    sp.dma_start(xt[p][:, :, :], io["xT"].rearrange("(g p) (b t) -> p g b t", p=P, b=B)[:, :, m, bass.ds(turn * P, P)]).then_inc(xt_in[p], 16)
                    wait_apart(sp, mem, (z_ready, 4 * (n - 1)))
                    sp.dma_start(gr[p][:, :].rearrange("k (h t) -> k h t", h=H),
                                 mem["g_parts"][:, 32 * m:32 * m + H, bass.ds(turn * P, P)]).then_inc(gr_in[p], 16)

                four_steps(sp, LO, ML, MH, NT, body)
                for e in range(E8 + 1):
                    for dst, src in ((mem["Win"], io["w_in"]), (mem["Wsw"], io["w_sw"])):
                        sp.dma_start(dst[:, e, :, :], src[e].rearrange("(g p) f -> p g f", p=P)).then_inc(ex_in, 16)
                sp.wait_ge(init, 3)
                for k in range(8):
                    r = NI * P // 8
                    sp.dma_start(mem["rows"][k * r:(k + 1) * r, :].rearrange("(a p) d -> p a d", p=P),
                                 zero[:, :].unsqueeze(1).to_broadcast([P, r // P, D])).then_inc(ex_in, 16)
                sp.wait_ge(ex_in, 16 * (2 * (E8 + 1) + 8))

            def run(e, body):
                four_steps(e, LO, ML, MH, HI, body)

            @block.tensor
            def _(pe):
                pe.wait_ge(w_in, 16 * 11)
                pe.wait_ge(init, 3)

                def gates(n, m, turn, r):
                    if r == 0:
                        pe.wait_ge(gr_in[m % 2], 16 * (2 * turn + m // 2 + 1))
                    wait(pe, d_done, 4 * n + r - 1)
                    pe.matmul(bZ[r % 2][:, :], ones3[:, :], gr[m % 2][:, r * 512:(r + 1) * 512],
                              start=True, stop=True).then_inc(z_ready, 1)

                def scores(i, m, r):
                    p = (m - 1) % 2
                    if r == 0:
                        pe.wait_ge(phi_done, i + 1)
                        pe.wait_ge(km_done, i + 1)
                    wait(pe, a_done, 4 * i + r - 1)
                    for g in range(G):
                        for e in range(2):
                            mm = pe.matmul(bS[r % 2][:, (2 * g + e) * P:(2 * g + e + 1) * P],
                                           kh[p][32 * r:32 * r + 32, e, g, :], qk[p][32 * r:32 * r + 32, 0, g, :],
                                           start=True, stop=True)
                    mm.then_inc(s_ready, 1)

                def values(i, m, r):
                    p = (m - 1) % 2
                    if r == 0:
                        pe.wait_ge(v_read, i + 1)
                    pe.wait_ge(a_done, 4 * i + r + 1)
                    for j in range(4 * r, 4 * r + 4):
                        mm = pe.matmul(bM1[:, D + j * DH:D + (j + 1) * DH], A[:, j, :], vt[p][:, j * DH:(j + 1) * DH],
                                       start=True, stop=True)
                    mm.then_inc(av_done, 1)

                def body(n, m, turn):
                    i, p1 = n - 1, (m - 1) % 2
                    if has(n, 0):
                        p = m % 2
                        pe.wait_ge(xt_in[p], 16 * (2 * turn + m // 2 + 1))
                        wait(pe, qk_read, QK_READS * n)
                        for o in range(4):
                            for g in range(G):
                                mm = pe.matmul(bQK[:, o * P:(o + 1) * P], Wqk[:, g, o * P:(o + 1) * P], xt[p][:, g, :],
                                               start=(g == 0), stop=(g == G - 1))
                        mm.then_inc(qk_ready, 1)
                        if has(n, 7):
                            wait(pe, xnt_read, n - 6)
                        elif has(n, 3):
                            wait(pe, yt_read, n - 2)
                        else:
                            wait(pe, v_read, n)
                        for g in range(G):
                            mm = pe.matmul(bM0[:, 0:D], xt[p][:, g, :], Wv[:, g, :], start=(g == 0), stop=(g == G - 1))
                        mm.then_inc(v_ready, 1)
                    if has(n, 1):
                        scores(i, m, 0)
                    if has(n, 0):
                        gates(n, m, turn, 0)
                    if has(n, 1):
                        wait(pe, y_done, i)
                        for g in range(G):
                            mm = pe.transpose(bM1[:, g * P:(g + 1) * P], qk[p1][:, 1, g, :], ident[:, :])
                        mm.then_inc(kt_ready, 1)
                    if has(n, 2):
                        j = n - 2
                        if has(n, 0):
                            pe.wait_ge(v_read, n + 1)
                        pe.wait_ge(y_done, j + 1)
                        if not has(n, 0) and has(n, 7):
                            wait(pe, xnt_read, n - 6)
                        for g in range(G):
                            mm = pe.transpose(bM0[:, g * P:(g + 1) * P], y[:, g * P:(g + 1) * P], ident[:, :])
                        mm.then_inc(yt_ready, 1)
                    if has(n, 1):
                        scores(i, m, 1)
                    if has(n, 0):
                        gates(n, m, turn, 1)
                    if has(n, 1):
                        pe.wait_ge(kw_done, 2 * (i + 1))
                        wait(pe, st_step, 2 * (i - 3))
                        yv = bM1[:, 0:D].rearrange("p (r g c) -> p g r c", r=4, g=G)
                        for g in range(G):
                            mm = pe.matmul(yv[:, g], qk[p1][:, 0, g, :],
                                           St[:, (m - 1) % 4, g, :].rearrange("p (r c) -> p r c", r=4), start=True, stop=True)
                        mm.then_inc(y2_done, 1)
                        values(i, m, 0)
                    if has(n, 2):
                        wait(pe, um_done, n - 1)
                        if has(n, 7):
                            wait(pe, r_read, n - 6)
                        pe.wait_ge(yt_read, n - 1)
                        for g in range(G):
                            mm = pe.matmul(bM2[:, 0:D], yT[:, g, :], Wo[:, g, :], start=(g == 0), stop=(g == G - 1))
                        mm.then_inc(o_ready, 1)
                    if has(n, 6):
                        pe.wait_ge(xn_done, n - 5)
                        if has(n, 2):
                            pe.wait_ge(yt_read, n - 1)
                        else:
                            wait(pe, xnt_read, n - 6)
                        for g in range(G):
                            mm = pe.transpose(bM0[:, g * P:(g + 1) * P], xn[m % 2][:, g * P:(g + 1) * P], ident[:, :])
                        mm.then_inc(xnt_ready, 1)
                    for r in (2, 3):
                        if has(n, 1):
                            scores(i, m, r)
                        if has(n, 0):
                            gates(n, m, turn, r)
                        if has(n, 1):
                            values(i, m, r - 1)
                    if has(n, 1):
                        values(i, m, 3)
                    if has(n, 2):
                        pe.wait_ge(res_done, n - 1)
                    if has(n, 1):
                        for g in range(G):
                            mm = pe.matmul(bM2[:, g * P:(g + 1) * P], kw[:, g * P:(g + 1) * P],
                                           vt[p1][:, :].rearrange("p (r g c) -> p g r c", r=4, g=G)[:, g], start=True, stop=True)
                        mm.then_inc(u_ready, 1)
                    if has(n, 6):
                        pe.wait_ge(xnt_read, n - 5)
                        if not has(n, 2):
                            wait(pe, r_read, n - 6)
                        for g in range(G):
                            mm = pe.matmul(bM2[:, D:D + E8], xnT[:, g, :], Wr[:, g, :], start=(g == 0), stop=(g == G - 1))
                        mm.then_inc(r_ready, 1)

                run(pe, body)

            @block.scalar
            def _(act):
                def body(n, m, turn):
                    if has(n, 0):
                        act.wait_ge(qk_ready, n + 1)
                        wait(act, phi_done, n)
                        act.activation(eqk[:, 0:D], bQK[:, 0:D], ACT.Exp, scale=0.25).then_inc(act_phi, 1)
                        act.activation(eqk[:, D:2 * D], bQK[:, D:2 * D], ACT.Exp).then_inc(act_phi, 1)
                        act.activation(rqk[:, 0:D], bQK[:, 0:D], ACT.Relu, scale=0.25).then_inc(qk_read, 1)
                        act.activation(rqk[:, D:2 * D], bQK[:, D:2 * D], ACT.Relu).then_inc(qk_read, 1)
                        act.wait_ge(v_ready, n + 1)
                        wait(act, u_ready, n - 1)
                        act.activation(vt[m % 2][:, :], bM0[:, 0:D], ACT.Copy).then_inc(v_read, 1)
                    if has(n, 2):
                        act.wait_ge(yt_ready, n - 1)
                        wait(act, o_ready, n - 2)
                        act.activation(yT[:, :, :].rearrange("p g t -> p (g t)"), bM0[:, 0:D], ACT.Copy).then_inc(yt_read, 1)
                    if has(n, 6):
                        act.wait_ge(xnt_ready, n - 5)
                        wait(act, r_ready, n - 6)
                        act.activation(xnT[:, :, :].rearrange("p g t -> p (g t)"), bM0[:, 0:D], ACT.Copy).then_inc(xnt_read, 1)

                run(act, body)

            @block.vector
            def _(v):
                v.memset(ones3[:, :], 1.0).then_inc(init, 1)
                v.memset(St[:, :, :, :], 0.0).then_inc(init, 1)
                v.memset(zero[:, :], 0.0).then_inc(init, 1)
                v.wait_ge(w_in, 16 * 11)

                def weigh(i, m, r):
                    v.wait_ge(s_ready, 4 * i + r + 1)
                    wait(v, av_done, 4 * (i - 1) + r + 1)
                    v.wait_ge(d_done, 4 * i + r + 1)
                    v.tensor_tensor(A[:, 4 * r:4 * r + 4, :], bS[r % 2][:, :].rearrange("p (h t) -> p h t", h=4),
                                    dcy[(m - 1) % 2][:, 4 * r:4 * r + 4, :], ALU.mult).then_inc(a_done, 1)

                def decay(n, m, r):
                    v.wait_ge(z_ready, 4 * n + r + 1)
                    wait(v, a_done, 4 * (n - 2) + r + 1)
                    wait(v, kw_done, 2 * (n - 1))
                    for h in range(4):
                        ins = v.tensor_tensor_scan(dcy[m % 2][:, 4 * r + h, :], bZ[r % 2][:, h * P:(h + 1) * P], ident[:, :],
                                                   0.0, ALU.mult, ALU.add)
                    ins.then_inc(d_done, 1)

                def body(n, m, turn):
                    i = n - 1
                    if has(n, 2):
                        j = n - 2
                        cj = turn if m >= 2 else turn - 1
                        bj = (m - 2) % 4
                        v.wait_ge(av_done, 4 * (j + 1))
                        v.wait_ge(y2_done, j + 1)
                        v.tensor_tensor(ye[:, :].rearrange("p (h c) -> p h c", h=H), bM1[:, 0:D].rearrange("p (h c) -> p h c", h=H),
                                        mem["Etok"][:, bass.ds(cj, 1), 32 * bj:32 * bj + H].rearrange("p o h -> p (o h)").unsqueeze(2).to_broadcast([P, H, DH]),
                                        ALU.mult).then_inc(ye_done, 1)
                        v.wait_ge(ye_done, j + 1)
                        wait(v, yt_ready, j)
                        v.tensor_tensor(y[:, :], bM1[:, D:2 * D], ye[:, :], ALU.add).then_inc(y_done, 1)
                        v.wait_ge(u_ready, j + 1)
                        if has(n, 7):
                            v.wait_ge(r_ready, n - 6)
                        wait(v, st_step, 2 * j)
                        v.tensor_tensor(um[:, :, :], bM2[:, 0:D].rearrange("p (g c) -> p g c", g=G), blk[:, :, :], ALU.mult).then_inc(um_done, 1)
                    if has(n, 7):
                        t = n - 7
                        v.wait_ge(r_ready, t + 1)
                        v.tensor_copy(mem["score"][:, bass.ds(t, 1), :].rearrange("p o e -> p (o e)"), bM2[:, D:D + E8]).then_inc(r_read, 1)
                    if has(n, 6):
                        t, q = n - 6, (m - 6) % 4
                        grp = turn - 1 if m >= 2 else turn - 2
                        v.wait_ge(nw, NWT * (grp + 1))
                        wait(v, xnt_ready, t - 1)
                        wait(v, xc_done, t - 1)
                        v.tensor_scalar(xn[m % 2][:, :], X[:, bass.ds(t, 1), :].rearrange("p o d -> p (o d)"), mv[:, q, 0:1], rstd[:, q:q + 1],
                                        ALU.subtract, ALU.mult).then_inc(xn_done, 1)
                    if has(n, 1):
                        weigh(i, m, 0)
                    if has(n, 0):
                        decay(n, m, 0)
                    if has(n, 1):
                        v.wait_ge(kt_ready, i + 1)
                        wait(v, u_ready, i)
                        v.wait_ge(d_done, 4 * i + 4)
                        dl = dcy[(m - 1) % 2][:, :, P - 1:P].rearrange("p (r g e) o -> p g r (e o)", r=4, g=G)
                        for g in range(G):
                            v.tensor_tensor(kw[:, g * P:(g + 1) * P].rearrange("p (r e c) -> p r e c", r=4, e=2),
                                            bM1[:, g * P:(g + 1) * P].rearrange("p (r e c) -> p r e c", r=4, e=2),
                                            dl[:, g].unsqueeze(3).to_broadcast([P, 4, 2, DH]), ALU.mult).then_inc(kw_done, 1)
                    for r in (1, 2, 3):
                        if has(n, 1):
                            weigh(i, m, r)
                        if has(n, 0):
                            decay(n, m, r)
                        if r == 2 and has(n, 0):
                            v.wait_ge(act_phi, 2 * (n + 1))
                            v.wait_ge(qk_read, QK_READS * (n + 1))
                            wait(v, u_ready, n - 1)
                            wait(v, km_done, n - 1)
                            v.scalar_tensor_tensor(out=qk[m % 2][:, :, :, :].rearrange("p a g t -> p (a g t)"), in0=eqk[:, :], scalar=1.0,
                                                   in1=rqk[:, :], op0=ALU.min, op1=ALU.add).then_inc(phi_done, 1)
                    if has(n, 2):
                        j, q = n - 2, (m - 2) % 4
                        xj = X[:, bass.ds(j, 1), :].rearrange("p o d -> p (o d)")
                        v.wait_ge(o_ready, j + 1)
                        v.tensor_tensor(xj, bM2[:, 0:D], xj, ALU.add).then_inc(res_done, 1)
                        wait_apart(v, mem, (res_done, j + 1), (ag_done, j))
                        v.bn_stats(stat[:, :], xj).then_inc(bn_done, 1)
                        wait_apart(v, mem, (bn_done, j + 1), (xn_done, j - 3))
                        v.bn_aggr(mv[:, q, :], stat[:, :]).then_inc(ag_done, 1)
                        if q == 3:
                            grp = turn - 1
                            v.wait_ge(ag_done, j + 1)
                            rsqrt_group(v, nw, NWT * grp, mv[:, :, 1], nt[:, :], na[:, :], rstd[:, :])

                run(v, body)
                v.wait_ge(r_read, NT)
                for t in range(NT):
                    v.max(mem["topv"][:, t, :], mem["score"][:, t, :]).then_inc(mx_done, 1)
                for t in range(NT):
                    v.wait_ge(mx_done, t + 1)
                    v.max_index(mem["topi"][:, t, :], mem["topv"][:, t, :], mem["score"][:, t, :]).then_inc(mi_done, 1)
                v.wait_ge(mi_done, NT)

            @block.gpsimd
            def _(pool):
                pool.wait_ge(w_in, 16 * 11)
                pool.wait_ge(init, 3)

                def body(n, m, turn):
                    if has(n, 2):
                        j, bj = n - 2, (m - 2) % 4
                        ti = turn if m >= 2 else turn - 1
                        wait_apart(pool, mem, (st_step, 2 * j))
                        pool.tensor_tensor(Sd[:, :, :], St[:, bj, :, :],
                                           mem["dec"][:, :, bass.ds(ti + bj * NC, 1)].to_broadcast([P, G, P]), ALU.mult).then_inc(sd_done, 1)
                        pool.wait_ge(um_done, j + 1)
                        pool.wait_ge(y2_done, j + 1)
                        pool.wait_ge(sd_done, j + 1)
                        pool.tensor_tensor(St[:, bj, :, :], Sd[:, :, :], um[:, :, :], ALU.add).then_inc(st_step, 2)
                    if has(n, 0):
                        wait_apart(pool, mem, (s_ready, 4 * (n - 1)), (phi_done, n + 1))
                        for e in range(2):
                            ins = pool.tensor_scalar(kh[m % 2][:, e, :, :], qk[m % 2][:, 1, :, :], hmask[:, e:e + 1], None, ALU.mult)
                        ins.then_inc(km_done, 1)
                    if has(n, 6):
                        t = n - 6
                        pool.wait_ge(xn_done, t + 1)
                        pool.tensor_copy(X[:, bass.ds(t, 1), :].rearrange("p o d -> p (o d)"), xn[m % 2][:, :]).then_inc(xc_done, 1)

                run(pool, body)
                pool.wait_ge(xc_done, NT)


def build_shared_and_routes(nc, io, mem):
    X = mem["X"]
    with ExitStack() as c2:
        def sb(name, shape, dt=F32):
            return c2.enter_context(nc.sbuf_tensor("r_" + name, shape, dt))

        def sem(name):
            return c2.enter_context(nc.semaphore("r_" + name))

        iota8 = sb("iota8", [P, E8])
        item = sb("item", [P, NI])
        tri = sb("tri", [P, P])
        ones = sb("ones", [P, P])
        ones8 = sb("ones8", [P, NT])
        idx_f = [sb(f"idx_f{k}", [P, NT]) for k in range(2)]
        pick = [sb(f"pick{k}", [P, NT, E8]) for k in range(2)]
        both = sb("both", [P, NT, E8])
        total = sb("total", [P, NT, E8])
        incl = sb("incl", [P, NT, E8])
        off = sb("off", [P, NT, E8])
        tmp = sb("tmp", [P, NT, E8])
        slot_f = sb("slot_f", [P, NT])
        cnt = sb("cnt", [P, E8])
        cnt_i = sb("cnt_i", [P, E8], I32)
        cnt_s = sb("cnt_s", [P, E8], I32)
        tiles = sb("tiles", [P, E8])
        ends = sb("ends", [P, E8])
        base = sb("base", [P, E8])
        cmp = sb("cmp", [1, NI, E8])
        exf = sb("exf", [1, NI])
        gate = sb("gate", [P, NT, 2])
        row = [[sb(f"row{p}{k}", [P, D]) for k in range(2)] for p in range(2)]
        rix = [[sb(f"rix{p}{k}", [P, 1], U32) for k in range(2)] for p in range(2)]
        bR = c2.enter_context(nc.psum_tensor("r_bR", [P, 2, 512], F32))

        w_in, dve, counted, gate_ready, cuts = sem("w_in"), sem("dve"), sem("counted"), sem("gate_ready"), sem("cuts")
        wo_in = [sem("wo_in"), sem("wo_sh_in")]
        row_ready, rix_ready = sem("row_ready"), sem("rix_ready")
        sent = [[sem(f"sent{p}{k}") for k in range(2)] for p in range(2)]

        def route(v):
            n = 0

            def link(ins):
                nonlocal n
                n += 1
                ins.then_inc(dve, 1)
                v.wait_ge(dve, n)

            v.wait_ge(w_in, 16 * 3)
            v.memset(ones[:, :], 1.0).then_inc(cuts, 1)
            link(v.memset(ones8[:, :], 1.0))
            for k in range(2):
                link(v.tensor_copy(idx_f[k][:, :], mem["topi"][:, :, k]))
                link(v.tensor_tensor(pick[k][:, :, :], iota8[:, :].unsqueeze(1).to_broadcast([P, NT, E8]),
                                     idx_f[k][:, :].unsqueeze(2).to_broadcast([P, NT, E8]), ALU.is_equal))
            v.tensor_tensor(both[:, :, :], pick[0][:, :, :], pick[1][:, :, :], ALU.add).then_inc(cuts, 1)
            v.wait_ge(counted, 1)
            link(v.tensor_copy(total[:, :, :], bR[:, 1, 0:NT * E8].rearrange("p (t e) -> p t e", e=E8)))
            for e in range(E8):
                link(v.tensor_tensor_scan(incl[:, :, e], ones8[:, :], total[:, :, e], 0.0, ALU.mult, ALU.add))
            link(v.tensor_scalar(cnt[:, :], incl[:, NT - 1, :], float(P - 1), None, ALU.add))
            link(v.tensor_copy(cnt_i[:, :], cnt[:, :]))
            link(v.tensor_scalar(cnt_s[:, :], cnt_i[:, :], 7, None, ALU.arith_shift_right))
            link(v.tensor_copy(tiles[:, :], cnt_s[:, :]))
            link(v.tensor_tensor_scan(ends[:, :], ones8[:, 0:E8], tiles[:, :], 0.0, ALU.mult, ALU.add))
            link(v.tensor_tensor(base[:, :], ends[:, :], tiles[:, :], ALU.subtract))
            link(v.tensor_scalar(base[:, :], base[:, :], float(P), None, ALU.mult))
            link(v.tensor_tensor(off[:, :, :], incl[:, :, :], total[:, :, :], ALU.subtract))
            link(v.tensor_tensor(off[:, :, :], off[:, :, :], bR[:, 0, 0:NT * E8].rearrange("p (t e) -> p t e", e=E8), ALU.add))
            link(v.tensor_tensor(off[:, :, :], off[:, :, :], base[:, :].unsqueeze(1).to_broadcast([P, NT, E8]), ALU.add))
            for k in range(2):
                link(v.tensor_tensor(tmp[:, :, :], pick[k][:, :, :], off[:, :, :], ALU.mult))
                link(v.tensor_reduce(slot_f[:, :], tmp[:, :, :], AX.X, ALU.add))
                link(v.tensor_copy(mem["slot"][:, k, :], slot_f[:, :]))
            link(v.tensor_tensor(cmp[:, :, :], item[0:1, :].unsqueeze(2).to_broadcast([1, NI, E8]),
                                 ends[0:1, :].unsqueeze(1).to_broadcast([1, NI, E8]), ALU.is_ge))
            link(v.tensor_reduce(exf[:, :], cmp[:, :, :], AX.X, ALU.add))
            link(v.tensor_scalar(exf[:, :], exf[:, :], float(E8 - 1), None, ALU.min))
            link(v.tensor_copy(mem["expert"][:, :], exf[:, :]))
            v.wait_ge(gate_ready, 1)

        def count(pe):
            pe.wait_ge(w_in, 16 * 3)
            pe.wait_ge(cuts, 2)
            pe.wait_ge(wo_in[1], 16)
            pe.matmul(bR[:, 0, 0:NT * E8], tri[:, :], both[:, :, :].rearrange("p t e -> p (t e)"), start=True, stop=True)
            pe.matmul(bR[:, 1, 0:NT * E8], ones[:, :], both[:, :, :].rearrange("p t e -> p (t e)"), start=True, stop=True).then_inc(counted, 1)

        def gates(act):
            act.activation(gate[:, :, :], mem["topv"][:, :, 0:2], ACT.Sigmoid).then_inc(gate_ready, 1)

        def dispatch_rows(v, t, m, turn):
            p = m % 2
            for k in range(2):
                if not (isinstance(t, int) and t < 2):
                    v.wait_ge(sent[p][k], 16 * (2 * turn + m // 2))
                v.tensor_scalar(row[p][k][:, :], X[:, bass.ds(t, 1), :].rearrange("p o d -> p (o d)"), gate[:, bass.ds(t, 1), k], None,
                                ALU.mult).then_inc(row_ready, 1)
                v.tensor_copy(rix[p][k][:, :], mem["slot"][:, k, bass.ds(t, 1)]).then_inc(rix_ready, 1)

        def dispatch_send(pool, t, m, turn):
            p = m % 2
            wait_apart(pool, mem, (row_ready, 2 * (t + 1)), (rix_ready, 2 * (t + 1)))
            for k in range(2):
                pool.indirect_dma_start(out=mem["rows"], out_offset=bass.IndirectOffsetOnAxis(ap=rix[p][k][:, 0:1], axis=0),
                                        in_=row[p][k][:, :], in_offset=None).then_inc(sent[p][k], 16)

        def dispatch_end(pool):
            for p in range(2):
                for k in range(2):
                    pool.wait_ge(sent[p][k], 16 * NT // 2)

        def consts(sp):
            for dst, name in ((iota8, "iota8"), (item, "item"), (tri, "tri")):
                sp.dma_start(dst[:, :], io[name]).then_inc(w_in, 16)
            for e in range(E8, -1, -1):
                sp.dma_start(mem["Wout"][:, e, :, :], io["w_out"][e].rearrange("(g p) f -> p g f", p=P)).then_inc(wo_in[e == E8], 16)

        def out_weights(sp):
            sp.wait_ge(wo_in[0], 16 * E8)

        build_expert_tiles(nc, mem, "sh_", NT, shared=True, before={"sp": consts, "act": gates, "pe": count, "v": route},
                           each={"v": dispatch_rows, "pool": dispatch_send}, after={"pool": dispatch_end, "sp": out_weights})


def build_expert_tiles(nc, mem, name_, count, shared, before={}, each={}, after={}):
    X, ident, Win, Wsw, Wout = mem["X"], mem["ident"], mem["Win"], mem["Wsw"], mem["Wout"]
    with ExitStack() as c2:
        def sb(name, shape, dt=F32):
            return c2.enter_context(nc.sbuf_tensor(name_ + name, shape, dt))

        def sem(name):
            return c2.enter_context(nc.semaphore(name_ + name))

        def bank(name):
            return c2.enter_context(nc.psum_tensor(name_ + name, [P, 512], F32))

        xg = [sb(f"xg{p}", [P, D]) for p in range(2)]
        xT = [sb(f"xT{p}", [P, G, P]) for p in range(2)]
        sl = sb("sl", [P, F])
        h = sb("h", [P, F])
        hT = sb("hT", [P, F])
        yo = [sb(f"yo{p}", [P, D]) for p in range(2)]
        bX, bA, bB, bH, bO = bank("bX"), bank("bA"), bank("bB"), bank("bH"), bank("bO")
        x_in, y_out = [sem("x_in0"), sem("x_in1")], [sem("y_out0"), sem("y_out1")]
        xt_ready, xt_read, mid_ready, sw_ready, silu_done, h_done, ht_ready, ht_read, o_ready, o_read = (
            sem(k) for k in ("xt_ready", "xt_read", "mid_ready", "sw_ready", "silu_done", "h_done", "ht_ready", "ht_read", "o_ready", "o_read"))

        def run(e, body):
            four_steps(e, 0, 4, count, count + 2, body)

        def has_(n, back):
            return has(n, back, count)

        with nc.Block() as block:
            @block.sync
            def _(sp):
                if "sp" in before:
                    before["sp"](sp)

                def body(n, m, turn):
                    if has_(n, 0):
                        p = m % 2
                        wait(sp, xt_ready, n - 1)
                        src = X[:, bass.ds(n, 1), :].rearrange("p o d -> p (o d)") if shared else mem["rows"][bass.ds(n * P, P), :]
                        sp.dma_start(xg[p][:, :], src).then_inc(x_in[p], 16)
                    if has_(n, 3) and not shared:
                        sp.wait_ge(o_read, n - 2)
                        sp.dma_start(mem["outs"][bass.ds((n - 3) * P, P), :], yo[(m - 3) % 2][:, :]).then_inc(y_out[(m - 3) % 2], 16)

                four_steps(sp, 0, 4, count, count + 3, body)
                if "sp" in after:
                    after["sp"](sp)
                if not shared:
                    for p in range(2):
                        sp.wait_ge(y_out[p], 16 * (count // 2))

            @block.tensor
            def _(pe):
                if "pe" in before:
                    before["pe"](pe)

                held = {}

                def expert_of(n, m, back):
                    if shared:
                        return E8
                    if back == 2 and m > 0 and m - 1 in held:
                        return held[m - 1]
                    e = pe.value_load(mem["expert"][0:1, bass.ds(n - back, 1)], min_val=0, max_val=E8 - 1)
                    if back == 1:
                        held[m] = e
                    return e

                def body(n, m, turn):
                    if m == 0:
                        held.clear()
                    if has_(n, 2):
                        pe.wait_ge(h_done, n - 1)
                        wait(pe, ht_read, n - 2)
                        for j in range(4):
                            mm = pe.transpose(bH[:, j * P:(j + 1) * P], h[:, j * P:(j + 1) * P], ident[:, :])
                        mm.then_inc(ht_ready, 1)
                    if has_(n, 0):
                        pe.wait_ge(x_in[m % 2], 16 * (2 * turn + m // 2 + 1))
                        wait(pe, xt_read, n)
                        for g in range(G):
                            mm = pe.transpose(bX[:, g * P:(g + 1) * P], xg[m % 2][:, g * P:(g + 1) * P], ident[:, :])
                        mm.then_inc(xt_ready, 1)
                    if has_(n, 1):
                        p = (m - 1) % 2
                        e = expert_of(n, m, 1)
                        pe.wait_ge(xt_read, n)
                        wait(pe, silu_done, n - 1)
                        for g in range(G):
                            mm = pe.matmul(bA[:, :], xT[p][:, g, :], Win[:, bass.ds(e, 1), g, :].rearrange("p o f -> p (o f)"),
                                           start=(g == 0), stop=(g == G - 1))
                        mm.then_inc(mid_ready, 1)
                        wait(pe, h_done, n - 1)
                        for g in range(G):
                            mm = pe.matmul(bB[:, :], xT[p][:, g, :], Wsw[:, bass.ds(e, 1), g, :].rearrange("p o f -> p (o f)"),
                                           start=(g == 0), stop=(g == G - 1))
                        mm.then_inc(sw_ready, 1)
                    if has_(n, 2):
                        e = expert_of(n, m, 2)
                        pe.wait_ge(ht_read, n - 1)
                        wait(pe, o_read, n - 2)
                        for j in range(4):
                            mm = pe.matmul(bO[:, 0:D], hT[:, j * P:(j + 1) * P], Wout[:, bass.ds(e, 1), j, :].rearrange("p o f -> p (o f)"),
                                           start=(j == 0), stop=(j == 3))
                        mm.then_inc(o_ready, 1)

                run(pe, body)

            @block.scalar
            def _(act):
                if "act" in before:
                    before["act"](act)

                def body(n, m, turn):
                    if has_(n, 0):
                        act.wait_ge(xt_ready, n + 1)
                        wait(act, sw_ready, n - 1)
                        act.activation(xT[m % 2][:, :, :].rearrange("p g t -> p (g t)"), bX[:, 0:D], ACT.Copy).then_inc(xt_read, 1)
                    if has_(n, 1):
                        act.wait_ge(mid_ready, n)
                        wait(act, h_done, n - 1)
                        act.activation(sl[:, :], bA[:, :], ACT.Silu).then_inc(silu_done, 1)
                    if has_(n, 2) and not shared:
                        act.wait_ge(o_ready, n - 1)
                        if not (isinstance(n, int) and n < 4):
                            act.wait_ge(y_out[m % 2], 16 * (2 * turn + m // 2 - 1))
                        act.activation(yo[m % 2][:, :], bO[:, 0:D], ACT.Copy).then_inc(o_read, 1)

                run(act, body)

            @block.vector
            def _(v):
                if "v" in before:
                    before["v"](v)

                def body(n, m, turn):
                    if has_(n, 2):
                        v.wait_ge(ht_ready, n - 1)
                        wait(v, o_ready, n - 2)
                        v.tensor_copy(hT[:, :], bH[:, :]).then_inc(ht_read, 1)
                    if has_(n, 0) and "v" in each:
                        each["v"](v, n, m, turn)
                    if has_(n, 1):
                        v.wait_ge(silu_done, n)
                        v.wait_ge(sw_ready, n)
                        wait(v, ht_ready, n - 1)
                        v.tensor_tensor(h[:, :], bB[:, :], sl[:, :], ALU.mult).then_inc(h_done, 1)
                    if has_(n, 2) and shared:
                        v.wait_ge(o_ready, n - 1)
                        xj = X[:, bass.ds(n - 2, 1), :].rearrange("p o d -> p (o d)")
                        v.tensor_tensor(xj, bO[:, 0:D], xj, ALU.add).then_inc(o_read, 1)

                run(v, body)
                if shared:
                    v.wait_ge(o_read, count)

            @block.gpsimd
            def _(pool):
                if "pool" in each:
                    four_steps(pool, 0, 4, count, count, lambda n, m, turn: each["pool"](pool, n, m, turn))
                if "pool" in after:
                    after["pool"](pool)


def build_combine(nc, mem):
    X = mem["X"]
    with ExitStack() as c2:
        def sb(name, shape, dt=F32):
            return c2.enter_context(nc.sbuf_tensor("c_" + name, shape, dt))

        def sem(name):
            return c2.enter_context(nc.semaphore("c_" + name))

        XT, ident = mem["XT"], mem["ident"]
        xs = [sb(f"xs{q}", [P, D]) for q in range(4)]
        bT = [c2.enter_context(nc.psum_tensor(f"c_bT{g}", [P, 512], F32)) for g in range(G)]
        xc_done, xt_ready, xt_read = sem("xc_done"), sem("xt_ready"), sem("xt_read")
        gix = [[sb(f"gix{p}{k}", [P, 1], U32) for k in range(2)] for p in range(4)]
        got = [[sb(f"got{p}{k}", [P, D]) for k in range(2)] for p in range(4)]
        stat, mv = sb("stat", [P, 6]), sb("mv", [P, 4, 2])
        nt, na, rstd = sb("nt", [P, 4]), sb("na", [P, 4]), sb("rstd", [P, 4])
        gix_ready, add1, add2, bn_done, ag_done, nw, xn_done = (sem(k) for k in ("gix_ready", "add1", "add2", "bn_done", "ag_done", "nw", "xn_done"))
        came = [[sem(f"came{p}{k}") for k in range(2)] for p in range(4)]

        with nc.Block() as block:
            @block.vector
            def _(v):
                def body(n, m, turn):
                    if has(n, 0):
                        for k in range(2):
                            wait(v, came[m][k], 16 * turn)
                            v.tensor_copy(gix[m][k][:, :], mem["slot"][:, k, bass.ds(n, 1)]).then_inc(gix_ready, 1)
                    if has(n, 3):
                        j, q = n - 3, (m - 3) % 4
                        xj = X[:, bass.ds(j, 1), :].rearrange("p o d -> p (o d)")
                        turn = turn + 1 if m == 3 else turn
                        v.wait_ge(came[q][0], 16 * turn)
                        v.tensor_tensor(xj, xj, got[q][0][:, :], ALU.add).then_inc(add1, 1)
                        v.wait_ge(add1, j + 1)
                        v.wait_ge(came[q][1], 16 * turn)
                        v.tensor_tensor(xj, xj, got[q][1][:, :], ALU.add).then_inc(add2, 1)
                        wait_apart(v, mem, (add2, j + 1), (ag_done, j))
                        v.bn_stats(stat[:, :], xj).then_inc(bn_done, 1)
                        wait_apart(v, mem, (bn_done, j + 1), (xn_done, j if q == 0 else 0))
                        v.bn_aggr(mv[:, q, :], stat[:, :]).then_inc(ag_done, 1)
                        if q == 3:
                            v.wait_ge(ag_done, j + 1)
                            rsqrt_group(v, nw, 12 * (turn - 1), mv[:, :, 1], nt[:, :], na[:, :], rstd[:, :])
                            v.wait_ge(nw, 12 * turn)
                            for qq in range(4):
                                xq = X[:, bass.ds(j - 3 + qq, 1), :].rearrange("p o d -> p (o d)")
                                wait(v, xt_ready, turn - 1)
                                wait(v, xc_done, 4 * (turn - 1))
                                v.tensor_scalar(xs[qq][:, :], xq, mv[:, qq, 0:1], rstd[:, qq:qq + 1], ALU.subtract, ALU.mult).then_inc(xn_done, 1)

                four_steps(v, 0, 8, NT, NT + 3, body)

            @block.tensor
            def _(pe):
                transpose_group(pe, NT // 4, xs, ident, bT, xn_done, xt_ready, xt_read)

            @block.scalar
            def _(act):
                def body(q):
                    keep_group(act, q, X, xs, xn_done, xc_done, lambda to, what: act.activation(to, what, ACT.Copy))
                    store_group(act, q, XT, bT, xt_ready, xt_read)

                blocks(act, NT // 4, body)
                act.wait_ge(xc_done, NT)

            @block.gpsimd
            def _(pool):
                def body(n, m, turn):
                    wait_apart(pool, mem, (gix_ready, 2 * (n + 1)), (add2, n - 3))
                    for k in range(2):
                        pool.indirect_dma_start(out=got[m][k][:, :], out_offset=None, in_=mem["outs"],
                                                in_offset=bass.IndirectOffsetOnAxis(ap=gix[m][k][:, 0:1], axis=0)).then_inc(came[m][k], 16)

                four_steps(pool, 0, 4, NT, NT, body)


def transpose_group(pe, groups, xs, ident, bT, xn_done, xt_ready, xt_read):
    def body(q):
        wait(pe, xt_read, 2 * q)
        for k in range(4):
            wait(pe, xn_done, 4 * q + k + 1)
            for g in range(G):
                mm = pe.transpose(bT[g][:, k * P:(k + 1) * P], xs[k][:, g * P:(g + 1) * P], ident[:, :])
        mm.then_inc(xt_ready, 1)

    blocks(pe, groups, body)


def store_group(act, q, XT, bT, xt_ready, xt_read):
    wait(act, xt_ready, q + 1)
    for g in range(G):
        act.activation(XT[:, g, bass.ds(q * 512, 512)], bT[g][:, :], ACT.Copy).then_inc(xt_read, 1)


def keep_group(e, q, X, xs, xn_done, xc_done, copy):
    e.wait_ge(xn_done, 4 * q + 4)
    for k in range(4):
        copy(X[:, bass.ds(4 * q + k, 1), :].rearrange("p o d -> p (o d)"), xs[k][:, :]).then_inc(xc_done, 1)


NB = NTOK // 512


def plane(pe, banks, W, rhs, col=0):
    for o in range(G):
        for i in range(G):
            mm = pe.matmul(banks[o][:, :], W[:, i, col + o * P:col + (o + 1) * P], rhs(i), start=(i == 0), stop=(i == G - 1))
    return mm


def build_memory_grad(nc, io, mem):
    XT, ident = mem["XT"], mem["ident"]
    with ExitStack() as c2:
        def sb(name, shape, dt=F32):
            return c2.enter_context(nc.sbuf_tensor("m_" + name, shape, dt))

        def sem(name):
            return c2.enter_context(nc.semaphore("m_" + name))

        def bank(name):
            return c2.enter_context(nc.psum_tensor("m_" + name, [P, 512], F32))

        Wk, Wv, W1, W2, W2T = (sb(k, [P, G, D]) for k in ("Wk", "Wv", "W1", "W2", "W2T"))
        Wlr = sb("Wlr", [P, G])
        lr_w = sb("lr_w", [P, G, P])
        ones = sb("ones", [P, P])
        zb = sb("zb", [P, 512], BF16)
        bias = sb("bias", [P, 4, G])
        blr = sb("blr", [P, 1])
        h0, h1, vb, s1, s2, sl, dv1, dv2, u, dz2, dz1 = (sb(k, [P, G, 512]) for k in ("h0", "h1", "vb", "s1", "s2", "sl", "dv1", "dv2", "u", "dz2", "dz1"))
        alr = sb("alr", [P, 512])
        tok = {k: sb("t_" + k, [P, 4, D]) for k in ("h0", "h1", "dz2", "dz1")}
        bsum = sb("bsum", [P, 4])
        btmp = sb("btmp", [P, 4])
        gw = [sb(f"gw{k}", [P, 512]) for k in range(2)]
        ga = sb("ga", [P, 512])
        PA, PB, PT = [bank("PA0"), bank("PA1")], [bank("PB0"), bank("PB1")], [bank("PT0"), bank("PT1")]
        gW = [bank("gW1"), bank("gW2")]
        w_in, init = sem("w_in"), sem("init")
        k_ready, k_read, v_ready, v_read, lr_ready, lr_read = (sem(k) for k in ("k_ready", "k_read", "v_ready", "v_read", "lr_ready", "lr_read"))
        z1_ready, s1_done, sl1_done, h1_done, w1_done, dv1_done = (sem(k) for k in ("z1_ready", "s1_done", "sl1_done", "h1_done", "w1_done", "dv1_done"))
        z2_ready, s2_done, sl2_done, u_done, t_done, dp_done, w2_done, dv2_done, dz2_done = (
            sem(k) for k in ("z2_ready", "s2_done", "sl2_done", "u_done", "t_done", "dp_done", "w2_done", "dv2_done", "dz2_done"))
        dh_ready, dh_done, dz1_done, bsum_done = sem("dh_ready"), sem("dh_done"), sem("dz1_done"), sem("bsum_done")
        t_ready, t_read, g_ready, upd = sem("t_ready"), sem("t_read"), sem("g_ready"), sem("upd")
        CNST = 0.1 * 2.0 / D

        T1, T2 = sb("T1", [P, G, 4 * D]), sb("T2", [P, 4 * D // P, D])
        raw = [T[:, :, :].rearrange("p g n -> p (g n)") for T in (T1, T2)]
        tern_w = [T[:, :, :].rearrange("p g n -> p (g n)") for T in mem["ternary"]]
        sums, gam = sb("sums", [P, 2]), sb("gam", [P, 2])
        tern_in, sums_done, mean_ready, gam_done, tern = (sem(k) for k in ("tern_in", "sums_done", "mean_ready", "gam_done", "tern"))

        with nc.Block() as block:
            @block.sync
            def _(sp):
                for dst, name in ((Wk, "m_Wk"), (Wv, "m_Wv"), (W1, "m_W1"), (W2, "m_W2"), (W2T, "m_W2T")):
                    sp.dma_start(dst[:, :, :], io[name].rearrange("(g p) n -> p g n", p=P)).then_inc(w_in, 16)
                sp.dma_start(bias[:, :, :], io["m_bias"]).then_inc(w_in, 16)
                sp.dma_start(Wlr[:, :], io["m_Wlr"]).then_inc(w_in, 16)
                sp.dma_start(blr[:, :], io["m_blr"]).then_inc(w_in, 16)
                sp.dma_start(T1[:, :, :], io["t_W1T"].rearrange("(g p) n -> p g n", p=P)).then_inc(tern_in, 16)
                sp.dma_start(T2[:, :, :], io["t_W2T"].rearrange("(g p) n -> p g n", p=P)).then_inc(tern_in, 16)

            @block.tensor
            def _(pe):
                pe.wait_ge(w_in, 16 * 8)
                pe.wait_ge(init, 5)
                for k in range(2):
                    pe.matmul(gW[k][:, :], zb[:, 0:P], zb[:, :], start=True, stop=False, skip_group_check=True)

                def keys(q):
                    wait(pe, sl1_done, 2 * q)
                    plane(pe, PA, Wk, lambda i: XT[:, i, bass.ds(q * 512, 512)]).then_inc(k_ready, 1)

                def targets(q):
                    wait(pe, sl2_done, 2 * q)
                    plane(pe, PB, Wv, lambda i: XT[:, i, bass.ds(q * 512, 512)]).then_inc(v_ready, 1)

                def rates(q):
                    wait(pe, t_read, 8 * q - 2)
                    for g in range(G):
                        mm = pe.matmul(PT[0][:, :], lr_w[:, g, :], XT[:, g, bass.ds(q * 512, 512)], start=(g == 0), stop=(g == G - 1))
                    mm.then_inc(lr_ready, 1)

                def body(q, last=False):
                    def turn_tok(src, done, need, count):
                        wait(pe, done, need)
                        wait(pe, t_read, 2 * (4 * q + count))
                        if count == 0:
                            wait(pe, lr_read, q + 1)
                        if count == 3 and not last:
                            wait(pe, lr_read, q + 2)
                        for k in range(4):
                            for g in range(G):
                                mm = pe.transpose(PT[k // 2][:, (k % 2) * D + g * P:(k % 2) * D + (g + 1) * P],
                                                  src[:, g, k * P:(k + 1) * P], ident[:, :])
                        mm.then_inc(t_ready, 1)

                    def grad(k, left, right, need):
                        wait(pe, t_read, 2 * (4 * q + need))
                        for t in range(4):
                            for i in range(G):
                                mm = pe.matmul(gW[k][:, i * D:(i + 1) * D], tok[left][:, t, i * P:(i + 1) * P], tok[right][:, t, :],
                                               start=False, stop=False, skip_group_check=True)
                        mm.then_inc(g_ready, 1)

                    wait(pe, k_read, 2 * (q + 1))
                    wait(pe, dh_done, 2 * q)
                    plane(pe, PA, W1, lambda i: h0[:, i, :]).then_inc(z1_ready, 1)
                    turn_tok(h0, k_read, 2 * (q + 1), 0)
                    wait(pe, v_read, 2 * (q + 1))
                    wait(pe, h1_done, 2 * (q + 1))
                    plane(pe, PB, W2, lambda i: h1[:, i, :]).then_inc(z2_ready, 1)
                    turn_tok(h1, h1_done, 2 * (q + 1), 1)
                    if not last:
                        keys(q + 1)
                        wait(pe, k_read, 2 * (q + 2))
                    wait(pe, dz2_done, 2 * (q + 1))
                    wait(pe, sl1_done, 2 * (q + 1))
                    plane(pe, PA, W2T, lambda i: dz2[:, i, :]).then_inc(dh_ready, 1)
                    turn_tok(dz2, dz2_done, 2 * (q + 1), 2)
                    if not last:
                        targets(q + 1)
                    grad(1, "h1", "dz2", 3)
                    if not last:
                        rates(q + 1)
                    turn_tok(dz1, dz1_done, 2 * (q + 1), 3)
                    grad(0, "h0", "dz1", 4)

                keys(0)
                targets(0)
                rates(0)
                pe.wait_ge(sums_done, 2)
                pe.matmul(PT[1][:, 0:2], ones[:, :], sums[:, :], start=True, stop=True).then_inc(mean_ready, 1)
                pe.wait_ge(gam_done, 2)
                body(0)
                with pe.Fori(1, NB - 1) as q:
                    body(q)
                body(NB - 1, last=True)

            @block.scalar
            def _(act):
                act.wait_ge(w_in, 16 * 8)
                def keys(q):
                    wait(act, k_ready, q + 1)
                    wait(act, h1_done, 2 * q)
                    wait(act, t_ready, 4 * q - 3)
                    for g in range(G):
                        act.activation(h0[:, g, :], PA[g][:, :], ACT.Identity, bias=bias[:, 0, g:g + 1]).then_inc(k_read, 1)

                def targets(q):
                    wait(act, v_ready, q + 1)
                    wait(act, t_done, 2 * q)
                    for g in range(G):
                        act.activation(vb[:, g, :], PB[g][:, :], ACT.Identity, bias=bias[:, 1, g:g + 1]).then_inc(v_read, 1)

                def rates(q):
                    wait(act, lr_ready, q + 1)
                    wait(act, dp_done, 2 * q)
                    act.activation(alr[:, :], PT[0][:, :], ACT.Sigmoid, bias=blr[:, 0:1]).then_inc(lr_read, 1)

                def body(q, last=False):
                    def tok_copy(name, count):
                        wait(act, t_ready, 4 * q + count + 1)
                        wait(act, g_ready, 2 * q)
                        for k in range(2):
                            act.activation(tok[name][:, 2 * k:2 * k + 2, :].rearrange("p t d -> p (t d)"), PT[k][:, :], ACT.Copy).then_inc(t_read, 1)

                    wait(act, z1_ready, q + 1)
                    wait(act, w1_done, 2 * q)
                    wait(act, dv1_done, 2 * q)
                    for g in range(G):
                        act.activation(s1[:, g, :], PA[g][:, :], ACT.Sigmoid, bias=bias[:, 2, g:g + 1]).then_inc(s1_done, 1)
                    tok_copy("h0", 0)
                    wait(act, z2_ready, q + 1)
                    wait(act, w2_done, 2 * q)
                    wait(act, dv2_done, 2 * q)
                    for g in range(G):
                        act.activation(s2[:, g, :], PB[g][:, :], ACT.Sigmoid, bias=bias[:, 3, g:g + 1]).then_inc(s2_done, 1)
                    tok_copy("h1", 1)
                    if not last:
                        keys(q + 1)
                    tok_copy("dz2", 2)
                    if not last:
                        targets(q + 1)
                        rates(q + 1)
                    tok_copy("dz1", 3)

                keys(0)
                targets(0)
                rates(0)
                body(0)
                with act.Fori(1, NB - 1) as q:
                    body(q)
                body(NB - 1, last=True)

            @block.vector
            def _(v):
                v.memset(ones[:, :], 1.0).then_inc(init, 1)
                v.memset(zb[:, :], 0.0).then_inc(init, 1)
                v.memset(bsum[:, :], 0.0).then_inc(init, 1)
                v.wait_ge(w_in, 16 * 8)
                v.wait_ge(init, 3)
                for g in range(G):
                    v.tensor_scalar(lr_w[:, g, :], ones[:, :], Wlr[:, g:g + 1], None, ALU.mult).then_inc(init, 1)
                v.wait_ge(tern_in, 32)
                for k in range(2):
                    v.tensor_reduce(sums[:, k:k + 1], raw[k], AX.X, ALU.add, apply_absolute_value=True).then_inc(sums_done, 1)
                v.wait_ge(mean_ready, 1)
                v.tensor_scalar(gam[:, :], PT[1][:, 0:2], 1.0 / (4 * D * D), 1e-5, ALU.mult, ALU.add).then_inc(gam_done, 1)
                v.wait_ge(gam_done, 1)
                v.reciprocal(gam[:, :], gam[:, :]).then_inc(gam_done, 1)

                def body(q):
                    wait(v, s1_done, 2 * (q + 1))
                    for g in range(G):
                        v.scalar_tensor_tensor(out=sl[:, g, :], in0=PA[g][:, :], scalar=bias[:, 2, g:g + 1], in1=s1[:, g, :],
                                               op0=ALU.add, op1=ALU.mult).then_inc(sl1_done, 1)
                    wait(v, k_read, 2 * (q + 1))
                    wait(v, t_ready, 4 * q)
                    for g in range(G):
                        wait(v, sl1_done, 2 * q + g + 1)
                        v.tensor_tensor(h1[:, g, :], h0[:, g, :], sl[:, g, :], ALU.add).then_inc(h1_done, 1)
                    for g in range(G):
                        v.scalar_tensor_tensor(out=dv1[:, g, :], in0=s1[:, g, :], scalar=-1.0, in1=sl[:, g, :],
                                               op0=ALU.add, op1=ALU.mult).then_inc(w1_done, 1)
                    for g in range(G):
                        wait(v, w1_done, 2 * q + g + 1)
                        v.tensor_tensor(dv1[:, g, :], s1[:, g, :], dv1[:, g, :], ALU.subtract).then_inc(dv1_done, 1)
                    wait(v, v_read, 2 * (q + 1))
                    wait(v, h1_done, 2 * (q + 1))
                    wait(v, dz1_done, 2 * q)
                    for g in range(G):
                        v.tensor_tensor(u[:, g, :], h1[:, g, :], vb[:, g, :], ALU.subtract).then_inc(t_done, 1)
                    wait(v, s2_done, 2 * (q + 1))
                    wait(v, w1_done, 2 * (q + 1))
                    wait(v, h1_done, 2 * (q + 1))
                    for g in range(G):
                        v.scalar_tensor_tensor(out=sl[:, g, :], in0=PB[g][:, :], scalar=bias[:, 3, g:g + 1], in1=s2[:, g, :],
                                               op0=ALU.add, op1=ALU.mult).then_inc(sl2_done, 1)
                    for g in range(G):
                        wait(v, sl2_done, 2 * q + g + 1)
                        wait(v, t_done, 2 * q + g + 1)
                        v.tensor_tensor(u[:, g, :], u[:, g, :], sl[:, g, :], ALU.add).then_inc(u_done, 1)
                    wait(v, lr_read, q + 1)
                    for g in range(G):
                        wait(v, u_done, 2 * q + g + 1)
                        v.scalar_tensor_tensor(out=u[:, g, :], in0=u[:, g, :], scalar=CNST, in1=alr[:, :], op0=ALU.mult, op1=ALU.mult).then_inc(dp_done, 1)
                    for g in range(G):
                        v.scalar_tensor_tensor(out=dv2[:, g, :], in0=s2[:, g, :], scalar=-1.0, in1=sl[:, g, :],
                                               op0=ALU.add, op1=ALU.mult).then_inc(w2_done, 1)
                    for g in range(G):
                        wait(v, w2_done, 2 * q + g + 1)
                        v.tensor_tensor(dv2[:, g, :], s2[:, g, :], dv2[:, g, :], ALU.subtract).then_inc(dv2_done, 1)
                    wait(v, dh_ready, q)
                    wait(v, t_ready, 4 * q)
                    wait(v, bsum_done, q)
                    for g in range(G):
                        wait(v, dv2_done, 2 * q + g + 1)
                        wait(v, dp_done, 2 * q + g + 1)
                        v.tensor_tensor_reduce(dz2[:, g, :], u[:, g, :], dv2[:, g, :], 1.0, 0.0, ALU.mult, ALU.add,
                                               btmp[:, 2 + g:3 + g]).then_inc(dz2_done, 1)
                    wait(v, dh_ready, q + 1)
                    for g in range(G):
                        v.tensor_tensor(u[:, g, :], PA[g][:, :], u[:, g, :], ALU.add).then_inc(dh_done, 1)
                    for g in range(G):
                        wait(v, dh_done, 2 * q + g + 1)
                        wait(v, dv1_done, 2 * q + g + 1)
                        v.tensor_tensor_reduce(dz1[:, g, :], u[:, g, :], dv1[:, g, :], 1.0, 0.0, ALU.mult, ALU.add,
                                               btmp[:, g:g + 1]).then_inc(dz1_done, 1)
                    wait(v, dz1_done, 2 * (q + 1))
                    wait(v, dz2_done, 2 * (q + 1))
                    v.tensor_tensor(bsum[:, :], bsum[:, :], btmp[:, :], ALU.add).then_inc(bsum_done, 1)

                blocks(v, NB, body)

                n = 0

                def link(ins):
                    nonlocal n
                    n += 1
                    ins.then_inc(upd, 1)
                    v.wait_ge(upd, n)

                def adamw(new, was, gr):
                    a = ga[:, 0:gr.shape[1]]
                    link(v.scalar_tensor_tensor(out=a, in0=gr, scalar=-1.0, in1=gr, op0=ALU.mult, op1=ALU.max))
                    link(v.tensor_scalar(a, a, 1e-8, None, ALU.add))
                    link(v.reciprocal(a, a))
                    link(v.tensor_tensor(a, a, gr, ALU.mult))
                    link(v.tensor_scalar(a, a, -0.01, None, ALU.mult))
                    link(v.scalar_tensor_tensor(out=new, in0=was, scalar=1.0 - 0.01 * 0.01, in1=a, op0=ALU.mult, op1=ALU.add))

                v.wait_ge(g_ready, 2 * NB - 1)
                link(v.tensor_copy(gw[1][:, :], gW[1][:, :]))
                adamw(mem["W2n"][:, :, :].rearrange("p g d -> p (g d)"), W2[:, :, :].rearrange("p g d -> p (g d)"), gw[1][:, :])
                v.wait_ge(bsum_done, NB)
                adamw(mem["bn"][:, :, :].rearrange("p k g -> p (k g)"), bias[:, 2:4, :].rearrange("p k g -> p (k g)"), bsum[:, :])
                v.wait_ge(g_ready, 2 * NB)
                link(v.tensor_copy(gw[0][:, :], gW[0][:, :]))
                adamw(mem["W1n"][:, :, :].rearrange("p g d -> p (g d)"), W1[:, :, :].rearrange("p g d -> p (g d)"), gw[0][:, :])

            @block.gpsimd
            def _(pool):
                pool.wait_ge(gam_done, 2)
                for k in range(2):
                    pool.tensor_scalar(raw[k], raw[k], gam[:, k:k + 1], 1.0, ALU.mult, ALU.min).then_inc(tern, 1)
                for k in range(2):
                    pool.wait_ge(tern, k + 1)
                    pool.tensor_scalar(raw[k], raw[k], -1.0, 12582912.0, ALU.max, ALU.add).then_inc(tern, 1)
                for k in range(2):
                    pool.wait_ge(tern, k + 3)
                    pool.tensor_scalar(tern_w[k], raw[k], -12582912.0, 0.0, ALU.add, ALU.add).then_inc(tern, 1)
                pool.wait_ge(tern, 6)


def layer_norm_stats(v, mem, X, q, src, srcsem, sems, bufs):
    bn_done, ag_done, nw, xn_done = sems
    stat, mv, nt, na, rstd = bufs
    for k in range(4):
        xk = X[:, bass.ds(4 * q + k, 1), :].rearrange("p o d -> p (o d)")
        wait_apart(v, mem, (srcsem, src(k)), (ag_done, 4 * q))
        v.bn_stats(stat[:, k, :], xk).then_inc(bn_done, 1)
    wait_apart(v, mem, (bn_done, 4 * q + 4), (xn_done, 4 * q))
    for k in range(4):
        v.bn_aggr(mv[:, k, :], stat[:, k, :]).then_inc(ag_done, 1)


def layer_norm_apply(v, mem, X, q, sems, bufs, xs, before_xs):
    bn_done, ag_done, nw, xn_done = sems
    stat, mv, nt, na, rstd = bufs
    wait(v, ag_done, 4 * q + 4)
    rsqrt_group(v, nw, 12 * q, mv[:, :, 1], nt[:, :], na[:, :], rstd[:, :])
    wait(v, nw, 12 * q + 12)
    before_xs()
    for k in range(4):
        xk = X[:, bass.ds(4 * q + k, 1), :].rearrange("p o d -> p (o d)")
        v.tensor_scalar(xs[k][:, :], xk, mv[:, k, 0:1], rstd[:, k:k + 1], ALU.subtract, ALU.mult).then_inc(xn_done, 1)


def build_memory_read(nc, io, mem):
    X, XT, ident, W1n, W2n, bn = mem["X"], mem["XT"], mem["ident"], mem["W1n"], mem["W2n"], mem["bn"]
    with ExitStack() as c2:
        def sb(name, shape, dt=F32):
            return c2.enter_context(nc.sbuf_tensor("q_" + name, shape, dt))

        def sem(name):
            return c2.enter_context(nc.semaphore("q_" + name))

        def bank(name):
            return c2.enter_context(nc.psum_tensor("q_" + name, [P, 512], F32))

        Wq, bq = sb("Wq", [P, G, D]), sb("bq", [P, G])
        h0, h1, h2, s1, s2, sl, sm = (sb(k, [P, G, 512]) for k in ("h0", "h1", "h2", "s1", "s2", "sl", "sm"))
        xs = [sb(f"xs{k}", [P, D]) for k in range(4)]
        bufs = (sb("stat", [P, 4, 6]), sb("mv", [P, 4, 2]), sb("nt", [P, 4]), sb("na", [P, 4]), sb("rstd", [P, 4]))
        PA, PB, PT, PX = ([bank(f"{k}0"), bank(f"{k}1")] for k in ("PA", "PB", "PT", "PX"))
        w_in, q_ready, q_read, z1_ready, s1_done, sl1_done, h1_done = (sem(k) for k in ("w_in", "q_ready", "q_read", "z1_ready", "s1_done", "sl1_done", "h1_done"))
        z2_ready, s2_done, sl2_done, h2_done, t_ready, res_done = (sem(k) for k in ("z2_ready", "s2_done", "sl2_done", "h2_done", "t_ready", "res_done"))
        lns = [sem(k) for k in ("bn_done", "ag_done", "nw", "xn_done")]
        xn_done = lns[3]
        xc_done, xt_ready, xt_read = sem("xc_done"), sem("xt_ready"), sem("xt_read")

        def begun(q, back):
            return not isinstance(q, int) or q >= back

        with nc.Block() as block:
            @block.sync
            def _(sp):
                sp.dma_start(Wq[:, :, :], io["m_Wq"].rearrange("(g p) n -> p g n", p=P)).then_inc(w_in, 16)
                sp.dma_start(bq[:, :], io["m_bq"]).then_inc(w_in, 16)

            @block.tensor
            def _(pe):
                pe.wait_ge(w_in, 32)

                def front(q):
                    wait(pe, q_read, 2 * q)
                    plane(pe, PA, Wq, lambda i: XT[:, i, bass.ds(q * 512, 512)]).then_inc(q_ready, 1)

                def turn_h2(q):
                    pe.wait_ge(h2_done, 2 * (q + 1))
                    wait(pe, res_done, 2 * q)
                    for k in range(4):
                        for g in range(G):
                            mm = pe.transpose(PT[k // 2][:, (k % 2) * D + g * P:(k % 2) * D + (g + 1) * P], h2[:, g, k * P:(k + 1) * P], ident[:, :])
                    mm.then_inc(t_ready, 1)

                def turn_x(q):
                    wait(pe, xt_read, 2 * q)
                    for k in range(4):
                        pe.wait_ge(xn_done, 4 * q + k + 1)
                        for g in range(G):
                            mm = pe.transpose(PX[g][:, k * P:(k + 1) * P], xs[k][:, g * P:(g + 1) * P], ident[:, :])
                    mm.then_inc(xt_ready, 1)

                def body(q, last=False):
                    pe.wait_ge(q_read, 2 * (q + 1))
                    wait(pe, sl2_done, 2 * q)
                    plane(pe, PB, W1n, lambda i: h0[:, i, :]).then_inc(z1_ready, 1)
                    if begun(q, 1):
                        turn_h2(q - 1)
                    if begun(q, 2):
                        turn_x(q - 2)
                    pe.wait_ge(h1_done, 2 * (q + 1))
                    plane(pe, PB, W2n, lambda i: h1[:, i, :]).then_inc(z2_ready, 1)
                    if not last:
                        front(q + 1)

                front(0)
                for q in range(3):
                    body(q)
                with pe.Fori(3, NB - 1) as q:
                    body(q)
                body(NB - 1, last=True)
                turn_h2(NB - 1)
                turn_x(NB - 2)
                turn_x(NB - 1)

            @block.scalar
            def _(act):
                act.wait_ge(w_in, 32)

                def queries(q):
                    act.wait_ge(q_ready, q + 1)
                    wait(act, h1_done, 2 * q)
                    for g in range(G):
                        act.activation(h0[:, g, :], PA[g][:, :], ACT.Identity, bias=bq[:, g:g + 1]).then_inc(q_read, 1)

                def body(q, last=False):
                    act.wait_ge(z1_ready, q + 1)
                    for g in range(G):
                        act.activation(s1[:, g, :], PB[g][:, :], ACT.Sigmoid, bias=bn[:, 0, g:g + 1]).then_inc(s1_done, 1)
                    if begun(q, 2):
                        store_group(act, q - 2, XT, PX, xt_ready, xt_read)
                    act.wait_ge(z2_ready, q + 1)
                    for g in range(G):
                        act.activation(s2[:, g, :], PB[g][:, :], ACT.Sigmoid, bias=bn[:, 1, g:g + 1]).then_inc(s2_done, 1)
                    if not last:
                        queries(q + 1)

                queries(0)
                for q in range(2):
                    body(q)
                with act.Fori(2, NB - 1) as q:
                    body(q)
                body(NB - 1, last=True)
                store_group(act, NB - 2, XT, PX, xt_ready, xt_read)
                store_group(act, NB - 1, XT, PX, xt_ready, xt_read)

            @block.vector
            def _(v):
                def body(q):
                    v.wait_ge(s1_done, 2 * (q + 1))
                    for g in range(G):
                        v.scalar_tensor_tensor(out=sl[:, g, :], in0=PB[g][:, :], scalar=bn[:, 0, g:g + 1], in1=s1[:, g, :],
                                               op0=ALU.add, op1=ALU.mult).then_inc(sl1_done, 1)
                    wait(v, h2_done, 2 * q)
                    for g in range(G):
                        v.wait_ge(sl1_done, 2 * q + g + 1)
                        v.tensor_tensor(h1[:, g, :], h0[:, g, :], sl[:, g, :], ALU.add).then_inc(h1_done, 1)
                    if begun(q, 1):
                        residual(q - 1)
                    v.wait_ge(s2_done, 2 * (q + 1))
                    for g in range(G):
                        v.scalar_tensor_tensor(out=sm[:, g, :], in0=PB[g][:, :], scalar=bn[:, 1, g:g + 1], in1=s2[:, g, :],
                                               op0=ALU.add, op1=ALU.mult).then_inc(sl2_done, 1)
                    wait(v, t_ready, q)
                    for g in range(G):
                        v.wait_ge(sl2_done, 2 * q + g + 1)
                        v.tensor_tensor(h2[:, g, :], h1[:, g, :], sm[:, g, :], ALU.add).then_inc(h2_done, 1)
                    if begun(q, 1):
                        normalize(q - 1)

                def residual(q):
                    wait(v, t_ready, q + 1)
                    for k in range(2):
                        xk = X[:, bass.ds(4 * q + 2 * k, 2), :].rearrange("p o d -> p (o d)")
                        v.tensor_tensor(xk, PT[k][:, :], xk, ALU.add).then_inc(res_done, 1)
                    layer_norm_stats(v, mem, X, q, lambda k: 2 * q + k // 2 + 1, res_done, lns, bufs)

                def normalize(q):
                    def free():
                        wait(v, xt_ready, q)
                        wait(v, xc_done, 4 * q)

                    layer_norm_apply(v, mem, X, q, lns, bufs, xs, free)

                body(0)
                body(1)
                with v.Fori(2, NB) as q:
                    body(q)
                residual(NB - 1)
                normalize(NB - 1)

            @block.gpsimd
            def _(pool):
                def body(q):
                    keep_group(pool, q, X, xs, xn_done, xc_done, pool.tensor_copy)

                blocks(pool, NB, body)
                pool.wait_ge(xc_done, NT)


def build_ternary_mlp(nc, io, mem, out):
    X, XT = mem["X"], mem["XT"]
    FC = 4 * D // P
    with ExitStack() as c2:
        def sb(name, shape, dt=F32):
            return c2.enter_context(nc.sbuf_tensor("t_" + name, shape, dt))

        def sem(name):
            return c2.enter_context(nc.semaphore("t_" + name))

        def bank(name):
            return c2.enter_context(nc.psum_tensor("t_" + name, [P, 512], F32))

        W1r, W2r = mem["ternary"]
        b1, b2 = sb("b1", [P, FC]), sb("b2", [P, D])
        xr = [sb(f"xr{p}", [P, 2, G, 512], F32R) for p in range(2)]
        hr = [sb(f"hr{p}", [P, 2, FC, 512], F32R) for p in range(2)]
        hf = [sb(f"hf{k}", [P, 512]) for k in range(2)]
        xo = [sb(f"xo{k}", [P, D]) for k in range(4)]
        bufs = (sb("stat", [P, 4, 6]), sb("mv", [P, 4, 2]), sb("nt", [P, 4]), sb("na", [P, 4]), sb("rstd", [P, 4]))
        bH, bO = [bank(f"bH{k}") for k in range(4)], [bank("bO0"), bank("bO1")]
        xh_done, xl_done, hl_done = sem("xh_done"), sem("xl_done"), sem("hl_done")
        w_in, h_ready, h_read, o_ready, o_read, b_done = (sem(k) for k in ("w_in", "h_ready", "h_read", "o_ready", "o_read", "b_done"))
        lns = [sem(k) for k in ("bn_done", "ag_done", "nw", "xn_done")]
        xn_done, y_out = lns[3], [sem(f"y_out{k}") for k in range(4)]

        with nc.Block() as block:
            @block.sync
            def _(sp):
                sp.dma_start(b1[:, :], io["t_b1"]).then_inc(w_in, 16)
                sp.dma_start(b2[:, :], io["t_b2"].rearrange("(o n) -> o n", o=1).to_broadcast([P, D])).then_inc(w_in, 16)
                def body(q):
                    for k in range(4):
                        wait(sp, xn_done, 4 * q + k + 1)
                        sp.dma_start(out[k, bass.ds(q * P, P), :], xo[k][:, :]).then_inc(y_out[k], 16)

                blocks(sp, NB, body)
                for k in range(4):
                    sp.wait_ge(y_out[k], 16 * NB)

            @block.tensor
            def _(pe):
                def up(q, p):
                    wait(pe, xh_done, q + 1)
                    wait(pe, xl_done, q + 1)
                    for f in range(FC):
                        wait(pe, h_read, FC * q + f - 3)
                        for g in range(G):
                            for part in range(2):
                                mm = pe.matmul(bH[f % 4][:, :], W1r[:, g, f * P:(f + 1) * P], xr[p][:, part, g, :],
                                               start=(g == 0 and part == 0), stop=(g == G - 1 and part == 1))
                        mm.then_inc(h_ready, 1)

                def down(q, p):
                    pe.wait_ge(hl_done, FC * (q + 1))
                    for k in range(4):
                        wait(pe, o_read, 4 * q + k - 1)
                        for f in range(FC):
                            for part in range(2):
                                mm = pe.matmul(bO[k % 2][:, 0:D], hr[p][:, part, f, k * P:(k + 1) * P], W2r[:, f, :],
                                               start=(f == 0 and part == 0), stop=(f == FC - 1 and part == 1))
                        mm.then_inc(o_ready, 1)

                up(0, 0)
                up(1, 1)
                down(0, 0)
                with pe.Fori(1, NB // 2) as j:
                    up(2 * j, 0)
                    down(2 * j - 1, 1)
                    up(2 * j + 1, 1)
                    down(2 * j, 0)
                down(NB - 1, 1)

            @block.scalar
            def _(act):
                act.wait_ge(w_in, 32)

                def x_hi(q, p):
                    wait(act, h_ready, FC * (q - 1))
                    wait(act, xl_done, q - 1)
                    act.activation(xr[p][:, 0, :, :], XT[:, :, bass.ds(q * 512, 512)], ACT.Copy).then_inc(xh_done, 1)

                def body(q, p, last=False):
                    wait(act, o_ready, 4 * (q - 1))
                    for f in range(FC):
                        act.wait_ge(h_ready, FC * q + f + 1)
                        wait(act, hl_done, FC * q + f - 1)
                        act.activation(hf[f % 2][:, :], bH[f % 4][:, :], ACT.Relu, bias=b1[:, f:f + 1])
                        act.activation(hr[p][:, 0, f, :], bH[f % 4][:, :], ACT.Relu, bias=b1[:, f:f + 1]).then_inc(h_read, 1)
                    if not last:
                        x_hi(q + 2, p)

                x_hi(0, 0)
                x_hi(1, 1)
                body(0, 0)
                body(1, 1)
                with act.Fori(1, NB // 2 - 1) as j:
                    body(2 * j, 0)
                    body(2 * j + 1, 1)
                body(NB - 2, 0, last=True)
                body(NB - 1, 1, last=True)

            @block.gpsimd
            def _(pool):
                def body(q, p):
                    for f in range(FC):
                        pool.wait_ge(h_read, FC * q + f + 1)
                        pool.tensor_tensor(hr[p][:, 1, f, :], hf[f % 2][:, :], hr[p][:, 0, f, :], ALU.subtract).then_inc(hl_done, 1)

                with pool.Fori(0, NB // 2) as j:
                    body(2 * j, 0)
                    body(2 * j + 1, 1)
                pool.wait_ge(hl_done, FC * NB)

            @block.vector
            def _(v):
                v.wait_ge(w_in, 32)

                def x_lo(q, p):
                    wait(v, xh_done, q + 1)
                    wait(v, h_ready, FC * (q - 1))
                    v.tensor_tensor(xr[p][:, 1, :, :], XT[:, :, bass.ds(q * 512, 512)], xr[p][:, 0, :, :], ALU.subtract).then_inc(xl_done, 1)

                def body(q, p, last=False):
                    if not last:
                        x_lo(q + 2, p)
                    for k in range(4):
                        xk = X[:, bass.ds(4 * q + k, 1), :].rearrange("p o d -> p (o d)")
                        v.tensor_tensor(xk, b2[:, :], xk, ALU.add).then_inc(b_done, 1)
                    for k in range(4):
                        xk = X[:, bass.ds(4 * q + k, 1), :].rearrange("p o d -> p (o d)")
                        wait(v, o_ready, 4 * q + k + 1)
                        wait(v, b_done, 4 * q + k + 1)
                        v.tensor_tensor(xk, bO[k % 2][:, 0:D], xk, ALU.add).then_inc(o_read, 1)

                    def free():
                        for k in range(4):
                            wait(v, y_out[k], 16 * q)

                    layer_norm_stats(v, mem, X, q, lambda k: 4 * q + k + 1, o_read, lns, bufs)
                    layer_norm_apply(v, mem, X, q, lns, bufs, xo, free)

                x_lo(0, 0)
                x_lo(1, 1)
                body(0, 0)
                body(1, 1)
                with v.Fori(1, NB // 2 - 1) as j:
                    body(2 * j, 0)
                    body(2 * j + 1, 1)
                body(NB - 2, 0, last=True)
                body(NB - 1, 1, last=True)


def rsqrt_group(v, sem, base, var, t, a, y):
    step = 0

    def link(ins):
        nonlocal step
        step += 1
        ins.then_inc(sem, 1)
        if step < 12:
            v.wait_ge(sem, base + step)

    link(v.tensor_scalar(t, var, EPS, None, ALU.add))
    link(v.tensor_scalar(a.bitcast(I32), t.bitcast(I32), 1, None, ALU.arith_shift_right))
    link(v.tensor_scalar(y.bitcast(I32), a.bitcast(I32), -1.0, float(0x5F3759DF), ALU.mult, ALU.add))
    for _ in range(3):
        link(v.tensor_tensor(a, y, y, ALU.mult))
        link(v.scalar_tensor_tensor(out=a, in0=a, scalar=-0.5, in1=t, op0=ALU.mult, op1=ALU.mult))
        link(v.scalar_tensor_tensor(out=y, in0=a, scalar=1.5, in1=y, op0=ALU.add, op1=ALU.mult))


def clear_released(nc):
    ids = sorted(nc.released_uncleared_semaphores)
    with nc.Block() as block:
        @block.gpsimd
        def _(pool):
            start = 0
            for k in range(1, len(ids) + 1):
                if k == len(ids) or ids[k] != ids[k - 1] + 1:
                    pool.sem_clear(range(ids[start], ids[k - 1] + 1))
                    start = k


def build(nc, io, out):
    with ExitStack() as ctx:
        def sb(name, shape, dt=F32):
            return ctx.enter_context(nc.sbuf_tensor(name, shape, dt))

        mem = {
            "X": sb("X", [P, NT, D]),
            "ident": sb("ident", [P, P]),
            "Etok": sb("Etok", [P, NC, P]),
            "dec": sb("dec", [P, G, B * NC]),
            "score": sb("score", [P, NT, E8]),
            "topv": sb("topv", [P, NT, E8]),
            "topi": sb("topi", [P, NT, E8], U32),
            "slot": sb("slot", [P, 2, NT], U32),
            "expert": sb("expert", [1, NI], I32),
            "rows": nc.dram_tensor("rows", (NI * P, D), F32, kind="Internal").ap(),
            "outs": nc.dram_tensor("outs", (NI * P, D), F32, kind="Internal").ap(),
            "g_parts": nc.dram_tensor("g_parts", (3, P, S), BF16, kind="Internal").ap(),
        }
        mem["begun"] = ctx.enter_context(nc.semaphore("begun"))
        build_gates(nc, ctx, io, mem)
        experts = ctx.enter_context(ExitStack())
        mem["Win"] = experts.enter_context(nc.sbuf_tensor("Win", [P, E8 + 1, G, F], F32))
        mem["Wsw"] = experts.enter_context(nc.sbuf_tensor("Wsw", [P, E8 + 1, G, F], F32))
        build_attention(nc, ctx, io, mem)
        mem["Wout"] = experts.enter_context(nc.sbuf_tensor("Wout", [P, E8 + 1, 4, D], F32))
        build_shared_and_routes(nc, io, mem)
        build_expert_tiles(nc, mem, "ro_", NI, shared=False)
        experts.close()
        clear_released(nc)
        mem["XT"] = sb("XT", [P, G, NTOK])
        mem["ternary"] = sb("W1r", [P, G, 4 * D], F32R), sb("W2r", [P, 4 * D // P, D], F32R)
        build_combine(nc, mem)
        mem["W1n"], mem["W2n"], mem["bn"] = sb("W1n", [P, G, D]), sb("W2n", [P, G, D]), sb("bn", [P, 2, G])
        build_memory_grad(nc, io, mem)
        build_memory_read(nc, io, mem)
        build_ternary_mlp(nc, io, mem, out)


def kernel(**inputs):
    import numpy as np
    import concourse.bacc as bacc
    from concourse import mybir as mb
    from concourse.bass_utils import run_bass_kernel_spmd as run

    a = {k: np.asarray(v) for k, v in inputs.items()}
    order = np.array([8 * g + 2 * r + e for r in range(4) for g in range(2) for e in range(2)])
    rows = (order[:, None] * DH + np.arange(DH)).reshape(-1)
    p = np.arange(P)
    hh = np.array([[(q // 32) * 4 + g * 2 + (q % 32) // 16 for q in range(P)] for g in range(G)])

    def columns(v):
        return v.reshape(-1, P).T

    arrays = {
        "x": a["L0_attn_x"],
        "xT": a["L0_attn_x"].reshape(NTOK, D).T,
        "WqT": a["L0_attn_Wq"].T, "WkT": a["L0_attn_Wk"].T,
        "WvT": a["L0_attn_Wv"][rows].T, "WoT": a["L0_attn_Wo"][:, rows].T,
        "WgT": a["L0_attn_Wg"][order].T, "bg": a["L0_attn_bg"][order],
        "router": a["L0_ffn_router_DE"],
        "w_in": np.concatenate([a["L0_ffn_w_in_eDF"], a["L0_ffn_w_in_shared_FD"].T[None]]),
        "w_sw": np.concatenate([a["L0_ffn_w_swiglu_eDF"], a["L0_ffn_w_swiglu_FD"].T[None]]),
        "w_out": np.concatenate([a["L0_ffn_w_out_eFD"], a["L0_ffn_w_out_shared_DF"].T[None]]),
        "m_Wk": a["L1_attn_Wk"], "m_Wv": a["L1_attn_Wv"], "m_Wq": a["L1_attn_Wq"], "m_W1": a["L1_attn_W1"], "m_W2": a["L1_attn_W2"],
        "m_W2T": a["L1_attn_W2"].T, "m_Wlr": columns(a["L1_attn_Wlr"][:, 0]), "m_blr": np.tile(a["L1_attn_blr"], (P, 1)), "m_bq": columns(a["L1_attn_bq"]),
        "m_bias": np.stack([columns(a[f"L1_attn_{k}"]) for k in ("bk", "bv", "b1", "b2")], axis=1),
        "t_W1T": a["L1_ffn_W1"].T, "t_W2T": a["L1_ffn_W2"].T, "t_b1": columns(a["L1_ffn_b1"]), "t_b2": a["L1_ffn_b2"],
        "iota8": np.tile(np.arange(E8, dtype=np.float32), (P, 1)),
        "item": np.tile(np.arange(NI, dtype=np.float32), (P, 1)),
        "tri": (p[:, None] < p[None, :]).astype(np.float32),
        "ident": np.eye(P, dtype=np.float32),
        "rep": np.stack([(p[:, None] % 32 == hh[g][None, :]) for g in range(G)]).astype(np.float32),
        "bmask": (p[:, None] // 32 == np.arange(B)[None, :]).astype(np.float32),
        "hmask": ((p[:, None] // 16) % 2 == np.arange(2)[None, :]).astype(np.float32),
        "blk": np.stack([(p[:, None] // 16 == p[None, :] // 16)] * G).astype(np.float32),
    }
    nc = bacc.Bacc("TRN2", target_bir_lowering=False, num_devices=1)
    io, feed = {}, {}
    for k, v in arrays.items():
        v = np.ascontiguousarray(v)
        feed[f"in_{k}"] = v
        io[k] = nc.dram_tensor(f"in_{k}", v.shape, mb.dt.from_np(v.dtype), kind="ExternalInput").ap()
    out = nc.dram_tensor("out", (B, S, D), F32, kind="ExternalOutput").ap()
    build(nc, io, out)
    r = run(nc, [feed], core_ids=[0])
    return r.results[0]["out"]
```
